# Optimizing a Trainium2 kernel written in Bass

```python
import numpy as np
import jax
import jax.numpy as jnp

def _softmax(x, axis=-1):
    return jax.nn.softmax(x, axis=axis)

def _gelu(x):
    return jax.nn.gelu(x, approximate=True)

def _silu(x):
    return jax.nn.silu(x)

def _sigmoid(x):
    return jax.nn.sigmoid(x)

def _layernorm(x, axis=-1, eps=1e-05):
    m = jnp.mean(x, axis=axis, keepdims=True)
    v = jnp.var(x, axis=axis, keepdims=True)
    return (x - m) / jnp.sqrt(v + eps)

def _scatter_add(tgt, idx, src, axis=0):
    return tgt.at[idx].add(src)

def _segment_sum(src, seg, n):
    return jax.ops.segment_sum(src, seg, n)
kernel_name = 'mk_seq_preln_d1_jaxref_r8_187753'

def setup_inputs(seed: int=0):
    np.random.seed(seed)
    _w = jnp.asarray

    def _L0_attn_setup():
        import jax, jax.numpy as jnp
        import numpy as np
        N, L, D_IN, H, HD, D_OUT = (4, 256, 128, 16, 64, 128)
        DIM = H * HD
        key = jax.random.key(seed)
        ks = jax.random.split(key, 5)
        s_in = 1.0 / np.sqrt(D_IN)
        s_d = 1.0 / np.sqrt(DIM)
        return {'data': jax.random.normal(ks[0], (N, L, D_IN), jnp.float32), 'W_qkv': jax.random.uniform(ks[1], (D_IN, 3 * DIM), jnp.float32, -s_in, s_in), 'b_qkv': jax.random.uniform(ks[2], (3 * DIM,), jnp.float32, -s_in, s_in), 'W_out': jax.random.uniform(ks[3], (DIM, D_OUT), jnp.float32, -s_d, s_d), 'b_out': jax.random.uniform(ks[4], (D_OUT,), jnp.float32, -s_d, s_d)}
    _L0_attn_in = _L0_attn_setup()

    def _L0_ffn_setup():
        import jax, jax.numpy as jnp
        import numpy as np
        E = 8
        H = 128
        M = 256
        K = 2
        SE = 1
        BSZ, SEQ = (2, 128)
        W_SCALE = 0.02
        key = jax.random.key(seed)
        ks = jax.random.split(key, 9)
        return {'x': jax.random.normal(ks[0], (BSZ, SEQ, H), jnp.float32), 'gate_w': jax.random.normal(ks[1], (E, H), jnp.float32) * W_SCALE, 'beta': jnp.zeros((E,), jnp.float32), 'gate_proj_w': jax.random.normal(ks[2], (E, H, M), jnp.float32) * W_SCALE, 'up_proj_w': jax.random.normal(ks[3], (E, H, M), jnp.float32) * W_SCALE, 'down_proj_w': jax.random.normal(ks[4], (E, M, H), jnp.float32) * W_SCALE, 'shared_gate_w': jax.random.normal(ks[5], (SE, H, M), jnp.float32) * W_SCALE, 'shared_up_w': jax.random.normal(ks[6], (SE, H, M), jnp.float32) * W_SCALE, 'shared_down_w': jax.random.normal(ks[7], (SE, M, H), jnp.float32) * W_SCALE}
    _L0_ffn_in = _L0_ffn_setup()
    _d = {'L0_attn_data': _L0_attn_in['data'], 'L0_attn_W_qkv': _L0_attn_in['W_qkv'], 'L0_attn_b_qkv': _L0_attn_in['b_qkv'], 'L0_attn_W_out': _L0_attn_in['W_out'], 'L0_attn_b_out': _L0_attn_in['b_out'], 'L0_ffn_gate_w': _L0_ffn_in['gate_w'], 'L0_ffn_beta': _L0_ffn_in['beta'], 'L0_ffn_gate_proj_w': _L0_ffn_in['gate_proj_w'], 'L0_ffn_up_proj_w': _L0_ffn_in['up_proj_w'], 'L0_ffn_down_proj_w': _L0_ffn_in['down_proj_w'], 'L0_ffn_shared_gate_w': _L0_ffn_in['shared_gate_w'], 'L0_ffn_shared_up_w': _L0_ffn_in['shared_up_w'], 'L0_ffn_shared_down_w': _L0_ffn_in['shared_down_w']}
    _x0 = _d['L0_attn_data']
    _d['L0_attn_data'] = jax.random.normal(jax.random.fold_in(jax.random.key(seed), 1), (8, 512, 128), dtype=_x0.dtype)
    del _x0
    return _d

def reference(L0_attn_data, L0_attn_W_qkv, L0_attn_b_qkv, L0_attn_W_out, L0_attn_b_out, L0_ffn_gate_w, L0_ffn_beta, L0_ffn_gate_proj_w, L0_ffn_up_proj_w, L0_ffn_down_proj_w, L0_ffn_shared_gate_w, L0_ffn_shared_up_w, L0_ffn_shared_down_w):

    def _L0_attn_ref(data, W_qkv, b_qkv, W_out, b_out):
        import jax, jax.numpy as jnp
        import numpy as np
        N, L, D_IN, H, HD, D_OUT = (4, 256, 128, 16, 64, 128)
        DIM = H * HD
        n, l = (data.shape[0], data.shape[1])
        qkv = data @ W_qkv + b_qkv
        q = qkv[:, :, :DIM].reshape(n, l, H, HD)
        k = qkv[:, :, DIM:2 * DIM].reshape(n, l, H, HD)
        v = qkv[:, :, 2 * DIM:].reshape(n, l, H, HD)
        scores = jnp.einsum('nqhd,nkhd->nhqk', q, k)
        attention = jax.nn.softmax(scores / jnp.sqrt(jnp.float32(HD)), axis=3)
        out = jnp.einsum('nhql,nlhd->nqhd', attention, v).reshape(n, l, DIM)
        return out @ W_out + b_out

    def _L0_ffn_ref(x, gate_w, beta, gate_proj_w, up_proj_w, down_proj_w, shared_gate_w, shared_up_w, shared_down_w):
        import jax, jax.numpy as jnp
        import numpy as np
        E = 8
        H = 128
        M = 256
        K = 2
        SE = 1
        BSZ, SEQ = (2, 128)
        W_SCALE = 0.02
        B0, S0, H0 = x.shape
        xt = x.reshape(-1, H0)
        B = xt.shape[0]
        logits = xt @ gate_w.T
        _, idx = jax.lax.top_k(logits + beta, K)
        probs = jax.nn.sigmoid(jnp.take_along_axis(logits, idx, axis=-1))
        c = jnp.zeros((B, E), xt.dtype).at[jnp.arange(B)[:, None], idx].add(probs)
        g = jnp.einsum('bh,ehm->bem', xt, gate_proj_w)
        u = jnp.einsum('bh,ehm->bem', xt, up_proj_w)
        h = jax.nn.silu(g) * u
        eo = jnp.einsum('bem,emh->beh', h, down_proj_w)
        combined = jnp.einsum('beh,be->bh', eo, c)
        sg = jnp.einsum('bh,ehm->bem', xt, shared_gate_w)
        su = jnp.einsum('bh,ehm->bem', xt, shared_up_w)
        sh = jax.nn.silu(sg) * su
        shared_out = jnp.einsum('bem,emh->beh', sh, shared_down_w).sum(axis=1)
        return (combined + shared_out).reshape(B0, S0, H0)
    x = L0_attn_data
    x = x + _L0_attn_ref(_layernorm(x, axis=-1), L0_attn_W_qkv, L0_attn_b_qkv, L0_attn_W_out, L0_attn_b_out)
    x = x + _L0_ffn_ref(_layernorm(x, axis=-1), L0_ffn_gate_w, L0_ffn_beta, L0_ffn_gate_proj_w, L0_ffn_up_proj_w, L0_ffn_down_proj_w, L0_ffn_shared_gate_w, L0_ffn_shared_up_w, L0_ffn_shared_down_w)
    return x

_drawn_inputs = setup_inputs


def setup_inputs(seed=0):
    import zlib

    import numpy as np

    out = dict(_drawn_inputs(seed))
    spreads = {'L0_ffn_beta': (0.0, 0.8)}
    factors = {'L0_attn_W_qkv': 3.154,
     'L0_attn_b_out': 3.063,
     'L0_ffn_gate_w': 8.0,
     'L0_ffn_gate_proj_w': 8.0,
     'L0_ffn_up_proj_w': 8.0,
     'L0_ffn_down_proj_w': 8.0,
     'L0_ffn_shared_gate_w': 6.906,
     'L0_ffn_shared_up_w': 6.82,
     'L0_ffn_shared_down_w': 6.831}
    for name, (base, spread) in spreads.items():
        noise = np.random.default_rng([zlib.crc32(name.encode()), seed]).standard_normal(out[name].shape)
        drawn = base * np.exp(spread * noise) if base else spread * noise
        out[name] = jnp.asarray(drawn.astype(out[name].dtype))
    for name, factor in factors.items():
        out[name] = (out[name] * factor).astype(out[name].dtype)
    return out
```

```python
import concourse.bass as bass
from concourse import mybir
from contextlib import ExitStack


def preln_attention_moe_kernel(
    nc, x_in, w_qkv, b_qkv, w_out, b_out, gate_w, beta, gate_proj, up_proj, down_proj,
    shared_gate, shared_up, shared_down, out,
):
    fp32, fp32r, fp16, u32 = mybir.dt.float32, mybir.dt.float32r, mybir.dt.float16, mybir.dt.uint32
    ALU, ACT, AX = mybir.AluOpType, mybir.ActivationFunctionType, mybir.AxisListType

    NB, L, D = x_in.shape
    P = 128
    T = NB * L
    NT = T // P
    HD = 64
    DIM = w_out.shape[0]
    NPAIR = DIM // (2 * HD)
    KT = L // P
    NE, M = gate_w.shape[0], gate_proj.shape[2]
    MT = M // P
    EX = NE + 1
    UNITS = NB * NPAIR
    EPS = 1e-5
    SCALE = float(HD) ** -0.5
    SHIFT = 32.0

    x_tok = x_in.rearrange("n (t p) d -> p (n t) d", p=P)
    out_tok = out.rearrange("n (t p) d -> p (n t) d", p=P)

    ctx = ExitStack()
    with ctx:
        def sb(name, shape, dt):
            return ctx.enter_context(nc.sbuf_tensor(name, shape, dt))

        def sem(name):
            return ctx.enter_context(nc.semaphore(name))

        def bank(name, cols=512):
            return ctx.enter_context(nc.psum_tensor(name, [P, cols], fp32))

        def wait(eng, s, n):
            if not isinstance(n, int) or n > 0:
                eng.wait_ge(s, n)

        x_res = sb("x_res", [P, NT, D], fp32)
        xT_hi = sb("xT_hi", [P, T], fp32r)
        xT_lo = sb("xT_lo", [P, T], fp32r)
        yT = sb("yT", [P, T], fp32)
        xn = yT[:, :].rearrange("p (t d) -> p t d", d=D)
        R1 = sb("R1", [P, 14336], fp32r)
        o = 0
        QK = 2 * 2 * L
        q1 = R1[:, 0:QK].rearrange("p (b h q) -> p b h q", b=2, h=2)
        k1 = R1[:, QK:2 * QK].rearrange("p (b h q) -> p b h q", b=2, h=2)
        q2 = R1[:, 2 * QK:3 * QK].rearrange("p (b h q) -> p b h q", b=2, h=2)
        k2 = R1[:, 3 * QK:4 * QK].rearrange("p (b h q) -> p b h q", b=2, h=2)
        o = 4 * QK
        wqk = R1[:, o:o + 4096].rearrange("p (r s d) -> p r s d", r=NPAIR, s=4)
        wv_hi = R1[:, o + 4096:o + 5120]
        wv_lo = R1[:, o + 5120:o + 6144]
        WEX = 2 * 2 * M + 2 * MT * D
        w_ex = [R1[:, e * WEX:(e + 1) * WEX] for e in range(EX)]
        cT = R1[:, EX * WEX:EX * WEX + L]
        wo = sb("wo", [P, NPAIR, 2, D], fp32r)
        R2 = sb("R2", [P, 4096], fp32r)
        nat = R2[:, 0:2048].rearrange("p (s q) -> p s q", s=4)
        oT = R2[:, 2048:3072].rearrange("p (s q) -> p s q", s=2)
        r_wqk = R2[:, 3072:3584].rearrange("p (s d) -> p s d", s=4)
        r_x = R2[:, 3584:3840].rearrange("p (s d) -> p s d", s=2)
        r_wo = R2[:, 3840:4096].rearrange("p (s d) -> p s d", s=2)
        h_sp = R2[:, :].rearrange("p (b s m q) -> p b s m q", b=2, s=2, m=MT)
        r_b = sb("r_b", [P, 2], fp32)
        r_vh = sb("r_vh", [P, KT, 2, HD + 1], fp16)
        r_vl = sb("r_vl", [P, KT, 2, HD], fp16)
        m_row = sb("m_row", [KT, 2, P], fp32r)
        e32 = sb("e32", [P, 2, 1024], fp32)
        prob = sb("prob", [P, 2, 2, KT, L], fp16)
        VW = 2 * KT * 2 * NPAIR
        v_all = sb("v_all", [P, VW * (2 * HD + 1)], fp16)
        v_hi = v_all[:, 0:VW * (HD + 1)].rearrange("p (t h d) -> p t h d", t=2 * KT, d=HD + 1)
        v_lo = v_all[:, VW * (HD + 1):].rearrange("p (t h d) -> p t h d", t=2 * KT, d=HD)
        v32 = v_all[:, :].bitcast(fp32)
        sq = prob[:, :, :, :, :].rearrange("p a b c d -> p (a b c d)").bitcast(fp32)
        o_sb = sb("o_sb", [P, KT, 2 * HD], fp32)
        mx = sb("mx", [P, 2, KT], fp32)
        rec = sb("rec", [P, KT], fp32)
        ident = sb("ident", [P, P], fp32)
        bqk = sb("bqk", [P, NPAIR, 2], fp32)
        bv = sb("bv", [P, NPAIR], fp32)
        bo = sb("bo", [P, 1], fp32)
        wb = sb("wb", [P, 1], fp32)
        mu = sb("mu", [P, NT], fp32)
        var = sb("var", [P, NT], fp32)
        rstd = sb("rstd", [P, NT], fp32)
        gwT = sb("gwT", [P, NE], fp32)
        beta_b = sb("beta_b", [P, NE], fp32)

        banks = [bank(f"bank{i}") for i in range(2)]
        s_bank = [bank(f"scores{i}", 1024) for i in range(2)]
        o_bank, x_bank = bank("o_bank"), bank("x_bank")

        s_x = [sem(f"x_in{g}") for g in range(4)]
        s_wraw, s_bias, s_small = sem("w_raw"), sem("bias_in"), sem("small_in")
        s_cst, s_wsp = sem("constants"), sem("w_split")
        s_wb = sem("wb_done")
        s_ln, s_sq, s_std = sem("ln_step"), sem("squared"), sem("std")
        s_tr, s_xh, s_xl = sem("x_transposed"), sem("x_hi"), sem("x_lo")
        GT = NT // 4

        raw_w = v32[:, 0:3 * DIM]
        raw_wo = v32[:, 3 * DIM:3 * DIM + NPAIR * D].rearrange("p (r d) -> p r d", r=NPAIR)

        def layernorm(dve, base, first):
            n = base
            for g in range(4):
                a, b = g * GT, (g + 1) * GT
                if first:
                    dve.wait_ge(s_x[g], 16)
                bc = lambda t: t[:, a:b].unsqueeze(2).to_broadcast([P, GT, D])
                dve.reduce_sum(mu[:, a:b], x_res[:, a:b, :], AX.X).then_inc(s_ln, 1)
                n += 1
                dve.wait_ge(s_ln, n)
                dve.tensor_scalar(mu[:, a:b], mu[:, a:b], 1.0 / D, None, ALU.mult).then_inc(s_ln, 1)
                n += 1
                dve.wait_ge(s_ln, n)
                dve.tensor_tensor(xn[:, a:b, :], x_res[:, a:b, :], bc(mu), ALU.subtract).then_inc(s_ln, 1)
                n += 1
            for g in range(4):
                a, b = g * GT, (g + 1) * GT
                bc = lambda t: t[:, a:b].unsqueeze(2).to_broadcast([P, GT, D])
                dve.wait_ge(s_sq, (0 if first else 4) + g + 1)
                dve.reduce_sum(var[:, a:b], sq[:, a * D:b * D].rearrange("p (t d) -> p t d", d=D), AX.X).then_inc(s_ln, 1)
                n += 1
                dve.wait_ge(s_ln, n)
                dve.tensor_scalar(var[:, a:b], var[:, a:b], 1.0 / D, EPS, ALU.mult, ALU.add).then_inc(s_ln, 1)
                n += 1
                dve.wait_ge(s_std, (0 if first else 4) + g + 1)
                dve.reciprocal(rstd[:, a:b], var[:, a:b]).then_inc(s_ln, 1)
                n += 1
                dve.wait_ge(s_ln, n)
                dve.tensor_tensor(xn[:, a:b, :], xn[:, a:b, :], bc(rstd), ALU.mult).then_inc(s_ln, 1)
                n += 1
            return n

        LN_STEPS = 4 * 3 + 4 * 4

        def layernorm_act(act, base, first):
            for g in range(4):
                act.wait_ge(s_ln, base + 3 * (g + 1))
                act.activation(sq[:, g * GT * D:(g + 1) * GT * D],
                               yT[:, g * GT * D:(g + 1) * GT * D], ACT.Square).then_inc(s_sq, 1)
            for g in range(4):
                act.wait_ge(s_ln, base + 12 + 4 * g + 2)
                act.activation(var[:, g * GT:(g + 1) * GT], var[:, g * GT:(g + 1) * GT],
                               ACT.Sqrt).then_inc(s_std, 1)

        def transpose_pe(pe, base, done):
            for b in range(NB):
                pe.wait_ge(s_ln, base + 12 + 4 * (b // 2 + 1))
                if done + b >= 2:
                    pe.wait_ge(s_xl, done + b - 1)
                for t in range(KT):
                    last = pe.transpose(banks[b % 2][:, t * P:(t + 1) * P], xn[:, KT * b + t, :], ident[:, :])
                last.then_inc(s_tr, 1)

        def transpose_hi(act, done):
            for b in range(NB):
                act.wait_ge(s_tr, done + b + 1)
                act.activation(xT_hi[:, b * L:(b + 1) * L], banks[b % 2][:, :], ACT.Copy).then_inc(s_xh, 1)

        def transpose_lo(dve, done):
            for b in range(NB):
                dve.wait_ge(s_xh, done + b + 1)
                dve.tensor_tensor(xT_lo[:, b * L:(b + 1) * L], banks[b % 2][:, :],
                                  xT_hi[:, b * L:(b + 1) * L], ALU.subtract).then_inc(s_xl, 1)

        with nc.Block() as block:
            @block.sync
            def _(sp):
                for g in range(4):
                    sp.dma_start(x_res[:, g * GT:(g + 1) * GT, :], x_tok[:, g * GT:(g + 1) * GT, :]).then_inc(s_x[g], 16)
                sp.dma_start(raw_w, w_qkv).then_inc(s_wraw, 16)
                sp.dma_start(raw_wo, w_out.rearrange("(r p) d -> p r d", p=P)).then_inc(s_wraw, 16)
                with nc.allow_non_contiguous_dma(reason="biases by partition"):
                    for s in range(2):
                        sp.dma_start(bqk[:, :, s], b_qkv[s * DIM:(s + 1) * DIM].rearrange("(r p) -> p r", p=P)).then_inc(s_bias, 16)
                    sp.dma_start(bv[:, :], b_qkv[2 * DIM:].rearrange("(r p) -> p r", p=P)).then_inc(s_bias, 16)
                    sp.dma_start(bo[:, :], b_out.rearrange("(p o) -> p o", o=1)).then_inc(s_bias, 16)
                    sp.dma_start(gwT[:, :], gate_w.rearrange("e h -> h e")).then_inc(s_small, 16)
                    sp.dma_start(beta_b[:, :], beta.rearrange("(o e) -> o e", o=1).to_broadcast([P, NE])).then_inc(s_small, 16)

            @block.gpsimd
            def _(pool):
                pool.memset(ident[:, :], 0.0).then_inc(s_cst, 1)
                pool.wait_ge(s_cst, 1)
                pool.affine_select(out=ident[:, :], in_=ident[:, :], compare_op=ALU.not_equal, fill=1.0,
                                   base=0, pattern=[[-1, P]], channel_multiplier=1).then_inc(s_cst, 1)
                pool.memset(k2[:, :, :, :].rearrange("p b h q -> p (b h q)").bitcast(fp32), 1.0).then_inc(s_cst, 1)
                pool.wait_ge(s_wraw, 32)
                wq3 = raw_w.rearrange("p (s r d) -> p s r d", s=3, r=NPAIR)
                parts = [(wqk[:, :, 0, :], wqk[:, :, 1, :], wq3[:, 0]), (wqk[:, :, 2, :], wqk[:, :, 3, :], wq3[:, 1]),
                         (wv_hi.rearrange("p (r d) -> p r d", r=NPAIR), wv_lo.rearrange("p (r d) -> p r d", r=NPAIR), wq3[:, 2]),
                         (wo[:, :, 0, :], wo[:, :, 1, :], raw_wo)]
                for hi, lo, raw in parts:
                    pool.tensor_copy(hi, raw).then_inc(s_wsp, 1)
                for n, (hi, lo, raw) in enumerate(parts):
                    pool.wait_ge(s_wsp, n + 1)
                    pool.tensor_tensor(lo, raw, hi, ALU.subtract).then_inc(s_wsp, 1)

            @block.vector
            def _(dve):
                layernorm(dve, 0, True)
                transpose_lo(dve, 0)
                dve.wait_ge(s_wb, 1)
                dve.wait_ge(s_bias, 64)
                dve.tensor_tensor(wb[:, :], x_bank[:, 0:1], bo[:, :], ALU.add).then_inc(s_cst, 1)

            @block.scalar
            def _(act):
                layernorm_act(act, 0, True)
                transpose_hi(act, 0)

            @block.tensor
            def _(pe):
                pe.wait_ge(s_cst, 2)
                transpose_pe(pe, 0, 0)
                pe.wait_ge(s_wraw, 32)
                pe.wait_ge(s_bias, 64)
                for r in range(NPAIR):
                    last = pe.matmul(x_bank[:, 0:1], raw_wo[:, r, :], bv[:, r:r + 1], start=(r == 0), stop=(r == NPAIR - 1))
                last.then_inc(s_wb, 1)

        names = ("q_done k_done v_done ot_done y_done mt_done max_mm s_mm pv_mm exp_done q_hi k_hi v_hi "
                 "o_hi mrow q_lo k_lo v_lo o_lo maxed o_norm o_rec y_acc p_lo q_put k_put m_put0 m_put1 ld_wqk ld_wo ld_x ld_v y_init v_ones")
        S = {n: sem(n) for n in names.split()}
        s_q, s_k, s_v, s_ot, s_y, s_mt = (S[n] for n in ("q_done", "k_done", "v_done", "ot_done", "y_done", "mt_done"))
        s_mm, s_sm, s_pv = S["max_mm"], S["s_mm"], S["pv_mm"]
        s_exp, s_qh, s_kh, s_vh, s_oh, s_mr = (S[n] for n in ("exp_done", "q_hi", "k_hi", "v_hi", "o_hi", "mrow"))
        s_ql, s_kl, s_vl, s_ol, s_mx, s_on, s_rec, s_ya = (
            S[n] for n in ("q_lo", "k_lo", "v_lo", "o_lo", "maxed", "o_norm", "o_rec", "y_acc"))
        s_pl, s_qp, s_kp, s_mp = S["p_lo"], S["q_put"], S["k_put"], (S["m_put0"], S["m_put1"])
        s_lw, s_lo, s_lx, s_lv = S["ld_wqk"], S["ld_wo"], S["ld_x"], S["ld_v"]
        s_yi, s_v1 = S["y_init"], S["v_ones"]
        CH = NPAIR
        PUT = 6 * 16

        def split3(pe, out_ap, sta_hi, sta_lo, mov_hi, mov_lo):
            pe.matmul(out_ap, sta_hi, mov_hi, start=True, stop=False)
            pe.matmul(out_ap, sta_hi, mov_lo, start=False, stop=False)
            return pe.matmul(out_ap, sta_lo, mov_hi, start=False, stop=True)

        def pe_q(pe, u, x_hi, x_lo):
            wait(pe, s_lw, 32 * (u + 1))
            wait(pe, s_mr, 2 * u)
            split3(pe, x_bank[:, :], r_wqk[:, 0], r_wqk[:, 1], x_hi, x_lo).then_inc(s_q, 1)

        def pe_k(pe, u, x_hi, x_lo):
            pe.wait_ge(s_ql, u + 1)
            split3(pe, x_bank[:, :], r_wqk[:, 2], r_wqk[:, 3], x_hi, x_lo).then_inc(s_k, 1)

        def pe_max(pe, u, par, h):
            if h == 0:
                pe.wait_ge(s_qp, PUT * (u + 1))
                pe.wait_ge(s_kp, PUT * (u + 1))
            for t in range(KT):
                g = 8 * u + 4 * h + t
                wait(pe, s_mx, g - 1)
                pe.matmul(banks[t % 2][:, :], q1[:, par, h, t * P:(t + 1) * P], k1[:, par, h, :],
                          start=True, stop=True).then_inc(s_mm, 1)

        def pe_mt(pe, u, h, before, n):
            wait(pe, before, n)
            pe.wait_ge(s_mx, 8 * u + 4 * h + 4)
            pe.transpose(x_bank[0:KT, 0:P], mx[:, h, :], ident[:, :]).then_inc(s_mt, 1)

        def pe_scores(pe, u, par, h, half):
            wait(pe, s_exp, 4 * u + 2 * h + half - 1)
            pe.wait_ge(s_mp[h], 16 * (u + 1))
            R = HD + 1
            for t in range(2):
                c = (2 * half + t) * P
                dst = s_bank[half][:, t * L:(t + 1) * L]
                pe.matmul(dst, k1[:, par, h, c:c + P], q1[:, par, h, :], start=True, stop=False)
                last = pe.matmul(dst, k2[0:R, par, h, c:c + P], q2[0:R, par, h, :], start=False, stop=True)
            last.then_inc(s_sm, 1)

        def pe_pv(pe, u, h):
            pe.wait_ge(s_pl, 4 * u + 2 * h + 2)
            pe.wait_ge(s_lv, 32 * (u + 1))
            wait(pe, s_on, 2 * u + h)
            for q in range(KT):
                dst = o_bank[:, q * (HD + 1):(q + 1) * (HD + 1)]
                for t in range(KT):
                    hi = prob[:, 0, h, t, q * P:(q + 1) * P]
                    lo = prob[:, 1, h, t, q * P:(q + 1) * P]
                    pe.matmul(dst, hi, r_vh[:, t, h, :], start=(t == 0), stop=False)
                    pe.matmul(dst[:, 0:HD], hi, r_vl[:, t, h, :], start=False, stop=False)
                    last = pe.matmul(dst, lo, r_vh[:, t, h, :], start=False, stop=(t == KT - 1))
            last.then_inc(s_pv, 1)

        def pe_ot(pe, u, before, n):
            wait(pe, before, n)
            pe.wait_ge(s_on, 2 * u + 2)
            for t in range(KT):
                last = pe.transpose(x_bank[:, t * P:(t + 1) * P], o_sb[:, t, :], ident[:, :])
            last.then_inc(s_ot, 1)

        def pe_y(pe, u):
            pe.wait_ge(s_ol, u + 1)
            pe.wait_ge(s_lo, 16 * (u + 1))
            split3(pe, x_bank[:, :], r_wo[:, 0], r_wo[:, 1], oT[:, 0], oT[:, 1]).then_inc(s_y, 1)

        def pe_v(pe, u, c, before, n):
            wait(pe, before, n)
            pe.wait_ge(s_lx, 32 * (u + 1))
            h = slice((c % 2) * L, (c % 2 + 1) * L)
            split3(pe, x_bank[:, :], r_x[:, 0], r_x[:, 1], wv_hi[:, h], wv_lo[:, h]).then_inc(s_v, 1)

        def x_of(u):
            n = u // NPAIR
            if isinstance(n, int):
                return xT_hi[:, n * L:(n + 1) * L], xT_lo[:, n * L:(n + 1) * L]
            return xT_hi[:, bass.ds(n * L, L)], xT_lo[:, bass.ds(n * L, L)]

        def pe_unit(pe, u, par, prev, nxt):
            pe_scores(pe, u, par, 0, 0)
            if prev:
                pe_pv(pe, u - 1, 1)
            if nxt:
                pe_q(pe, u + 1, *x_of(u + 1))
            pe_scores(pe, u, par, 0, 1)
            if nxt:
                pe_k(pe, u + 1, *x_of(u + 1))
            pe_scores(pe, u, par, 1, 0)
            if prev:
                pe_ot(pe, u - 1, *((s_kl, u + 2) if nxt else (s_mr, 2 * u + 2)))
            if nxt:
                pe_max(pe, u + 1, 1 - par, 0)
            pe_scores(pe, u, par, 1, 1)
            if prev:
                pe_y(pe, u - 1)
            if nxt:
                pe_max(pe, u + 1, 1 - par, 1)
            pe_pv(pe, u, 0)
            if nxt:
                pe_v(pe, u, par, *((s_ya, u) if prev else (s_kl, u + 2)))
                pe_mt(pe, u + 1, 0, s_vl, CH + u + 1)
                pe_mt(pe, u + 1, 1, s_mr, 2 * (u + 1) + 1)

        def act_exp(act, u, h, half):
            act.wait_ge(s_sm, 4 * u + 2 * h + half + 1)
            wait(act, s_pl, 4 * u + 2 * h + half - 1)
            if half == 0:
                wait(act, s_pv, 2 * u + h - 1)
            act.activation(e32[:, half, :], s_bank[half][:, :], ACT.Exp, scale=SCALE)
            dst = prob[:, 0, h, 2 * half:2 * half + 2, :].rearrange("p t q -> p (t q)")
            act.activation(dst, s_bank[half][:, :], ACT.Exp, scale=SCALE).then_inc(s_exp, 1)

        def act_hi(act, u, s, done, put, own):
            act.wait_ge(done, u + 1)
            wait(act, put, PUT * u)
            act.activation(nat[:, 2 * s], x_bank[:, :], ACT.Identity, bias=r_b[:, s:s + 1]).then_inc(own, 1)

        def act_oh(act, u):
            act.wait_ge(s_ot, u + 1)
            wait(act, s_y, u)
            act.activation(oT[:, 0], x_bank[:, :], ACT.Copy).then_inc(s_oh, 1)

        def v_slot(t, u, c):
            H = NPAIR
            if isinstance(u, int):
                at = ((u // NPAIR + 1) % 2) * KT + (u % NPAIR) // 2
                return t[:, at, c * H:(c + 1) * H, 0:HD]
            at = ((u // NPAIR + 1) % 2) * KT + (u % NPAIR) // 2
            return t[:, bass.ds(at, 1), c * H:(c + 1) * H, 0:HD].rearrange("p o h d -> p (o h) d")

        x3 = x_bank[:, :].rearrange("p (h d) -> p h d", d=HD)

        def act_vh(act, u, c):
            act.wait_ge(s_v, CH + u + 1)
            wait(act, s_lv, 32 * u)
            act.activation(v_slot(v_hi, u, c), x3, ACT.Copy).then_inc(s_vh, 1)

        def act_mr(act, u, h):
            act.wait_ge(s_mt, 2 * u + h + 1)
            wait(act, s_mp[h], 16 * u)
            act.activation(m_row[:, h, :], x_bank[0:KT, 0:P], ACT.Copy, bias=SHIFT, scale=-1.0).then_inc(s_mr, 1)

        def act_unit(act, u, par, prev, nxt):
            act_exp(act, u, 0, 0)
            if nxt:
                act_hi(act, u + 1, 0, s_q, s_qp, s_qh)
            act_exp(act, u, 0, 1)
            if nxt:
                act_hi(act, u + 1, 1, s_k, s_kp, s_kh)
            act_exp(act, u, 1, 0)
            if prev:
                act_oh(act, u - 1)
            act_exp(act, u, 1, 1)
            if nxt:
                act_vh(act, u, par)
                act_mr(act, u + 1, 0)
                act_mr(act, u + 1, 1)

        def dve_lo(dve, u, s, hi_done, put, own):
            dve.wait_ge(hi_done, u + 1)
            wait(dve, put, PUT * u)
            dve.scalar_tensor_tensor(out=nat[:, 2 * s + 1], in0=x_bank[:, :], scalar=r_b[:, s:s + 1],
                                     in1=nat[:, 2 * s].bitcast(fp32), op0=ALU.add, op1=ALU.subtract).then_inc(own, 1)

        def dve_max(dve, u, h):
            wait(dve, s_mt, 2 * u + h - 1)
            for t in range(KT):
                dve.wait_ge(s_mm, 8 * u + 4 * h + t + 1)
                dve.reduce_max(mx[:, h, t:t + 1], banks[t % 2][:, :], AX.X).then_inc(s_mx, 1)

        def dve_norm(dve, u, h):
            dve.wait_ge(s_pv, 2 * u + h + 1)
            wait(dve, s_on, 2 * u + h)
            o3 = o_bank[:, 0:KT * (HD + 1)].rearrange("p (q d) -> p q d", d=HD + 1)
            dve.reciprocal(rec[:, :].unsqueeze(2), o3[:, :, HD:HD + 1]).then_inc(s_rec, 1)
            dve.wait_ge(s_rec, 2 * u + h + 1)
            wait(dve, s_ot, u)
            dve.tensor_tensor(o_sb[:, :, h * HD:(h + 1) * HD], o3[:, :, 0:HD],
                              rec[:, :].unsqueeze(2).to_broadcast([P, KT, HD]), ALU.mult).then_inc(s_on, 1)

        def dve_ol(dve, u):
            dve.wait_ge(s_oh, u + 1)
            wait(dve, s_y, u)
            dve.tensor_tensor(oT[:, 1], x_bank[:, :], oT[:, 0].bitcast(fp32), ALU.subtract).then_inc(s_ol, 1)

        def dve_ya(dve, u):
            dve.wait_ge(s_y, u + 1)
            wait(dve, s_ya, u)
            n = u // NPAIR
            y = yT[:, n * L:(n + 1) * L] if isinstance(n, int) else yT[:, bass.ds(n * L, L)]
            dve.tensor_tensor(y, x_bank[:, :], y, ALU.add).then_inc(s_ya, 1)

        def dve_vl(dve, u, c):
            dve.wait_ge(s_vh, CH + u + 1)
            wait(dve, s_lv, 32 * u)
            dve.tensor_tensor(v_slot(v_lo, u, c), x3, v_slot(v_hi, u, c), ALU.subtract).then_inc(s_vl, 1)

        def dve_unit(dve, u, par, prev, nxt):
            if prev:
                dve_norm(dve, u - 1, 1)
            if nxt:
                dve_lo(dve, u + 1, 0, s_qh, s_qp, s_ql)
                dve_lo(dve, u + 1, 1, s_kh, s_kp, s_kl)
            if prev:
                dve_ol(dve, u - 1)
            if nxt:
                dve_max(dve, u + 1, 0)
            if prev:
                dve_ya(dve, u - 1)
            if nxt:
                dve_max(dve, u + 1, 1)
            dve_norm(dve, u, 0)
            if nxt:
                dve_vl(dve, u, par)

        def pool_unit(pool, u):
            for h in range(2):
                for half in range(2):
                    pool.wait_ge(s_exp, 4 * u + 2 * h + half + 1)
                    if half == 0:
                        wait(pool, s_pv, 2 * u + h - 1)
                    view = lambda s: prob[:, s, h, 2 * half:2 * half + 2, :].rearrange("p t q -> p (t q)")
                    pool.tensor_tensor(view(1), e32[:, half, :], view(0), ALU.subtract).then_inc(s_pl, 1)

        def move(eng, dst, src):
            if src.dtype == fp32r:
                dst, src = dst.bitcast(fp32), src.bitcast(fp32)
            return eng.dma_start(dst, src)

        def put_q(sp, u, par):
            sp.wait_ge(s_ql, u + 1)
            A, B = slice(0, HD), slice(HD, P)
            for h, src in ((0, A), (1, B)):
                for dst in (A, B):
                    move(sp, q1[dst, par, h, :], nat[src, 0]).then_inc(s_qp, 16)
                move(sp, q2[A, par, h, :], nat[src, 1]).then_inc(s_qp, 16)

        def put_k(sp, u, par):
            sp.wait_ge(s_kl, u + 1)
            A, B = slice(0, HD), slice(HD, P)
            for h, src in ((0, A), (1, B)):
                move(sp, k1[A, par, h, :], nat[src, 2]).then_inc(s_kp, 16)
                move(sp, k2[A, par, h, :], nat[src, 2]).then_inc(s_kp, 16)
                move(sp, k1[B, par, h, :], nat[src, 3]).then_inc(s_kp, 16)

        def put_m(sp, u, par, h):
            sp.wait_ge(s_mr, 2 * u + h + 1)
            move(sp, q2[HD:HD + 1, par, h, :], m_row[:, h, :]).then_inc(s_mp[h], 16)

        def at(t, n):
            return t[:, n:n + 1] if isinstance(n, int) else t[:, bass.ds(n, 1)]

        def ld_wqk(sp, u):
            wait(sp, s_k, u)
            wait(sp, s_kl, u)
            move(sp, r_wqk.rearrange("p (o s) d -> p o s d", o=1), at(wqk, u % NPAIR)).then_inc(s_lw, 16)
            move(sp, r_b[:, :].rearrange("p (o s) -> p o s", o=1), at(bqk, u % NPAIR)).then_inc(s_lw, 16)

        def ld_wo(sp, u):
            wait(sp, s_y, u)
            move(sp, r_wo.rearrange("p (o s) d -> p o s d", o=1), at(wo, u % NPAIR)).then_inc(s_lo, 16)

        def ld_x(sp, u):
            wait(sp, s_v, CH + u)
            t = ((u // NPAIR + 1) % NB) * KT + (u % NPAIR) // 2
            for s, src in enumerate((xT_hi, xT_lo)):
                x4 = src[:, :].rearrange("p (t d) -> p t d", d=P)
                move(sp, r_x[:, s:s + 1], at(x4, t)).then_inc(s_lx, 16)

        def ld_v(sp, u):
            n, r = u // NPAIR, u % NPAIR
            if isinstance(u, int) and u == 0:
                sp.wait_ge(s_vl, CH)
            wait(sp, s_pv, 2 * u)
            for ring, src in ((r_vh, v_hi), (r_vl, v_lo)):
                W = HD + 1 if ring is r_vh else HD
                flat = src.rearrange("p (b t) (r h) d -> p b r t (h d)", b=2, h=2)
                if isinstance(n, int):
                    s = flat[:, n % 2, r]
                else:
                    s = flat[:, bass.ds(n % 2, 1), bass.ds(r, 1)].rearrange("p a b t w -> p (a b t) w")
                move(sp, ring[:, :, :, :].rearrange("p t h d -> p t (h d)"), s).then_inc(s_lv, 16)

        def sp_unit(sp, u, par, prev, nxt):
            ld_v(sp, u)
            if nxt:
                put_q(sp, u + 1, 1 - par)
                put_k(sp, u + 1, 1 - par)
                if nxt > 1:
                    ld_wqk(sp, u + 2)
            ld_wo(sp, u)
            if nxt:
                put_m(sp, u + 1, 1 - par, 0)
                if nxt > 1:
                    ld_x(sp, u + 1)
                put_m(sp, u + 1, 1 - par, 1)

        def run_units(eng, step):
            step(eng, 0, 0, False, 2)
            step(eng, 1, 1, True, 2)
            with eng.Fori(1, UNITS // 2 - 1) as i:
                step(eng, 2 * i, 0, True, 2)
                step(eng, 2 * i + 1, 1, True, 2)
            step(eng, UNITS - 2, 0, True, 1)
            step(eng, UNITS - 1, 1, True, 0)

        with nc.Block() as block:
            @block.sync
            def _(sp):
                ld_wqk(sp, 0)
                sp.wait_ge(s_v1, 1)
                put_q(sp, 0, 0)
                put_k(sp, 0, 0)
                ld_wqk(sp, 1)
                ld_x(sp, 0)
                for h in range(2):
                    put_m(sp, 0, 0, h)
                run_units(sp, sp_unit)

            @block.gpsimd
            def _(pool):
                pool.memset(yT[:, :], 0.0).then_inc(s_yi, 1)
                pool.memset(v_hi[:, :, :, HD:HD + 1], 1.0).then_inc(s_v1, 1)
                run_units(pool, lambda pool, u, par, prev, nxt: pool_unit(pool, u))

            @block.scalar
            def _(act):
                act_hi(act, 0, 0, s_q, s_qp, s_qh)
                act_hi(act, 0, 1, s_k, s_kp, s_kh)
                for c in range(CH):
                    act.wait_ge(s_v, c + 1)
                    act.activation(v_hi[:, c // 2, (c % 2) * NPAIR:(c % 2 + 1) * NPAIR, 0:HD],
                                   s_bank[c % 2][:, 0:L].rearrange("p (h d) -> p h d", d=HD), ACT.Copy).then_inc(s_vh, 1)
                act_mr(act, 0, 0)
                act_mr(act, 0, 1)
                run_units(act, act_unit)
                act_oh(act, UNITS - 1)

            @block.vector
            def _(dve):
                dve_lo(dve, 0, 0, s_qh, s_qp, s_ql)
                dve_lo(dve, 0, 1, s_kh, s_kp, s_kl)
                for c in range(CH):
                    dve.wait_ge(s_vh, c + 1)
                    h = slice((c % 2) * NPAIR, (c % 2 + 1) * NPAIR)
                    dve.tensor_tensor(v_lo[:, c // 2, h, :], s_bank[c % 2][:, 0:L].rearrange("p (h d) -> p h d", d=HD),
                                      v_hi[:, c // 2, h, 0:HD], ALU.subtract).then_inc(s_vl, 1)
                dve_max(dve, 0, 0)
                dve_max(dve, 0, 1)
                dve.wait_ge(s_yi, 1)
                dve.tensor_scalar(yT[:, :], yT[:, :], wb[:, 0:1], None, ALU.add).then_inc(s_yi, 1)
                dve.wait_ge(s_yi, 2)
                run_units(dve, dve_unit)
                dve_norm(dve, UNITS - 1, 1)
                dve_ol(dve, UNITS - 1)
                dve_ya(dve, UNITS - 1)

            @block.tensor
            def _(pe):
                pe_q(pe, 0, *x_of(0))
                pe_k(pe, 0, *x_of(0))
                for c in range(CH):
                    if c >= 2:
                        pe.wait_ge(s_vl, c - 1)
                    t = slice((c // 2) * P, (c // 2 + 1) * P)
                    h = slice((c % 2) * L, (c % 2 + 1) * L)
                    split3(pe, s_bank[c % 2][:, 0:L], xT_hi[:, t], xT_lo[:, t], wv_hi[:, h], wv_lo[:, h]).then_inc(s_v, 1)
                pe.wait_ge(s_vl, CH)
                pe_max(pe, 0, 0, 0)
                pe_max(pe, 0, 0, 1)
                pe_mt(pe, 0, 0, s_kl, 1)
                pe_mt(pe, 0, 1, s_mr, 1)
                run_units(pe, pe_unit)
                U = UNITS
                pe_pv(pe, U - 1, 1)
                pe_ot(pe, U - 1, s_ya, U - 1)
                pe_y(pe, U - 1)

        s_yt, s_xr = sem("y_transposed"), sem("x_residual")
        s_lgT, s_lg8, s_lt, s_lg = sem("logitsT"), sem("logitsT_read"), sem("logits_transposed"), sem("logits_read")
        s_gws, s_rt, s_sg, s_wx, s_wxs, s_sel = (
            sem("gate_split"), sem("route_step"), sem("route_exp"), sem("expert_raw"), sem("expert_split"), sem("select"))
        RAW = 3 * M
        gsp = wo[:, 0:1, :, :].rearrange("p o s d -> p (o s) d")
        sel = wo[:, 1:5, :, :].rearrange("p r s d -> p (r s) d")
        lgT = o_sb[0:NE, :, :].rearrange("p t d -> p (t d)")
        small = e32[:, :, :].rearrange("p a b -> p (a b)")
        N8 = NT * NE
        lg, zb, mask, tmp, sig, cw = (small[:, j * N8:(j + 1) * N8].rearrange("p (t e) -> p t e", e=NE) for j in range(6))
        top = small[:, 6 * N8:7 * N8].rearrange("p (t e) -> p t e", e=NE)
        idx = small[:, 7 * N8:8 * N8].bitcast(u32).rearrange("p (t e) -> p t e", e=NE)
        cwk = sb("cwk", [P, NT, NE], fp32)
        c4 = sb("c4", [P, KT, NE], fp32)
        iota8 = sb("iota8", [P, NE], fp32)
        selw = sq[:, 0:NE * P].rearrange("p (e m) -> p e m", e=NE)

        with nc.Block() as block:
            @block.sync
            def _(sp):
                for e in range(EX):
                    g, u_, d_ = ((gate_proj[e], up_proj[e], down_proj[e]) if e < NE
                                 else (shared_gate[0], shared_up[0], shared_down[0]))
                    r = v32[:, e * RAW:(e + 1) * RAW]
                    sp.dma_start(r[:, 0:M], g).then_inc(s_wx, 16)
                    sp.dma_start(r[:, M:2 * M], u_).then_inc(s_wx, 16)
                    sp.dma_start(r[:, 2 * M:3 * M].rearrange("p (m d) -> p m d", m=MT),
                                 d_.rearrange("(m p) d -> p m d", p=P)).then_inc(s_wx, 16)

            @block.gpsimd
            def _(pool):
                pool.memset(gsp.rearrange("p s d -> p (s d)").bitcast(fp32), 0.0).then_inc(s_gws, 1)
                pool.wait_ge(s_gws, 1)
                pool.wait_ge(s_small, 32)
                pool.tensor_copy(gsp[:, 0, 0:NE], gwT[:, :]).then_inc(s_gws, 1)
                pool.wait_ge(s_gws, 2)
                pool.tensor_tensor(gsp[:, 1, 0:NE], gwT[:, :], gsp[:, 0, 0:NE].bitcast(fp32), ALU.subtract).then_inc(s_gws, 1)
                pool.iota(iota8[:, :], pattern=[[1, NE]], base=0, channel_multiplier=0,
                          allow_small_or_imprecise_dtypes=True).then_inc(s_gws, 1)
                pool.wait_ge(s_wx, 48 * EX)
                for e in range(EX):
                    raw = v32[:, e * RAW:(e + 1) * RAW].rearrange("p (s d) -> p s d", s=3)
                    w = w_ex[e].rearrange("p (s k d) -> p s k d", s=3, k=2)
                    pool.tensor_copy(w[:, :, 0, :], raw).then_inc(s_wxs, 1)
                    pool.wait_ge(s_wxs, 2 * e + 1)
                    pool.tensor_tensor(w[:, :, 1, :], raw, w[:, :, 0, :].bitcast(fp32), ALU.subtract).then_inc(s_wxs, 1)
                pool.memset(cT.bitcast(fp32), 0.0).then_inc(s_sel, 1)
                pool.wait_ge(s_ln, 2 * LN_STEPS)
                pool.memset(selw, 0.0).then_inc(s_sel, 1)
                for n, base in enumerate((0, -32)):
                    pool.wait_ge(s_sel, 2 + n)
                    pool.affine_select(out=selw, in_=selw, compare_op=ALU.not_equal, fill=1.0, base=base,
                                       pattern=[[-1, NE], [0, P]], channel_multiplier=1).then_inc(s_sel, 1)
                pool.wait_ge(s_sel, 4)
                pool.tensor_copy(sel, selw).then_inc(s_sel, 1)

            @block.vector
            def _(dve):
                for b in range(NB):
                    dve.wait_ge(s_yt, b + 1)
                    xs = x_res[:, KT * b:KT * (b + 1), :].rearrange("p t d -> p (t d)")
                    dve.tensor_tensor(xs, banks[b % 2][:, :], xs, ALU.add).then_inc(s_xr, 1)
                dve.wait_ge(s_xr, NB)
                layernorm(dve, LN_STEPS, False)
                transpose_lo(dve, NB)
                for b in range(NB):
                    dve.wait_ge(s_lgT, b + 1)
                    wait(dve, s_lt, b)
                    dve.tensor_copy(lgT, o_bank[0:NE, :]).then_inc(s_lg8, 1)
                    dve.wait_ge(s_lt, b + 1)
                    dve.tensor_copy(lg[:, KT * b:KT * (b + 1), :],
                                    x_bank[:, 0:KT * NE].rearrange("p (t e) -> p t e", e=NE)).then_inc(s_lg, 1)
                n = [0]

                def step(ins):
                    ins.then_inc(s_rt, 1)
                    n[0] += 1
                    dve.wait_ge(s_rt, n[0])

                dve.wait_ge(s_lg, NB)
                dve.wait_ge(s_small, 32)
                step(dve.tensor_tensor(zb, lg, beta_b[:, :].unsqueeze(1).to_broadcast([P, NT, NE]), ALU.add))
                for t in range(NT):
                    last = dve.max(top[:, t, :], zb[:, t, :])
                step(last)
                for t in range(NT):
                    last = dve.max_index(idx[:, t, :], top[:, t, :], zb[:, t, :])
                step(last)
                step(dve.tensor_copy(tmp, idx))
                dve.wait_ge(s_gws, 4)
                io = iota8[:, :].unsqueeze(1).to_broadcast([P, NT, NE])
                step(dve.tensor_tensor(mask, io, tmp[:, :, 0:1].to_broadcast([P, NT, NE]), ALU.is_equal))
                step(dve.tensor_tensor(top, io, tmp[:, :, 1:2].to_broadcast([P, NT, NE]), ALU.is_equal))
                step(dve.tensor_tensor(mask, mask, top, ALU.add))
                dve.wait_ge(s_sg, 1)
                step(dve.tensor_scalar(sig, sig, 1.0, None, ALU.add))
                step(dve.reciprocal(cw, sig))
                step(dve.tensor_tensor(cwk[:, :, :], cw, mask, ALU.mult))

            @block.scalar
            def _(act):
                layernorm_act(act, LN_STEPS, False)
                transpose_hi(act, NB)
                act.wait_ge(s_lg, NB)
                act.activation(sig, lg, ACT.Exp, scale=-1.0).then_inc(s_sg, 1)

            @block.tensor
            def _(pe):
                for b in range(NB):
                    if b >= 2:
                        pe.wait_ge(s_xr, b - 1)
                    for t in range(KT):
                        c = b * L + t * P
                        last = pe.transpose(banks[b % 2][:, t * P:(t + 1) * P], yT[:, c:c + P], ident[:, :])
                    last.then_inc(s_yt, 1)
                pe.wait_ge(s_xr, NB)
                transpose_pe(pe, LN_STEPS, NB)
                pe.wait_ge(s_gws, 3)
                for b in range(NB):
                    pe.wait_ge(s_xl, NB + b + 1)
                    wait(pe, s_lg8, b)
                    hi, lo = xT_hi[:, b * L:(b + 1) * L], xT_lo[:, b * L:(b + 1) * L]
                    pe.matmul(o_bank[:, :], gsp[:, 0], hi, start=True, stop=False)
                    pe.matmul(o_bank[:, :], gsp[:, 0], lo, start=False, stop=False)
                    pe.matmul(o_bank[:, :], gsp[:, 1], lo, start=False, stop=False)
                    pe.matmul(o_bank[:, :], gsp[:, 1], hi, start=False, stop=True).then_inc(s_lgT, 1)
                    pe.wait_ge(s_lg8, b + 1)
                    wait(pe, s_lg, b)
                    for t in range(KT):
                        last = pe.transpose(x_bank[:, t * NE:(t + 1) * NE], lgT[:, t * P:(t + 1) * P], ident[0:NE, 0:NE])
                    last.then_inc(s_lt, 1)

        names = ("c_copied c_transposed c_hi c_lo c_bcast c_read g_done u_done silu sc_done h_done h_hi h_lo "
                 "down_done y_read yt_done out_done out_put")
        S = {n: sem("m_" + n) for n in names.split()}
        m = S
        sl = yT[:, 0:2 * L].rearrange("p (m q) -> p m q", m=MT)
        sc = yT[:, 2 * L:4 * L].rearrange("p (m q) -> p m q", m=MT)
        hf = yT[:, 4 * L:6 * L].rearrange("p (m q) -> p m q", m=MT)
        cb = yT[:, 6 * L:8 * L].rearrange("p (b q) -> p b q", b=2)
        y_sb = sq[:, 2048:2048 + L]
        o_out = sq[:, 2560:2560 + 2 * L].rearrange("p (b q) -> p b q", b=2)
        g_bank = [s_bank[0][:, 0:L], s_bank[0][:, L:2 * L]]
        u_bank = [s_bank[1][:, 0:L], s_bank[1][:, L:2 * L]]
        c_bank, y_bank, t_bank = banks[0], banks[1], o_bank
        KC = 40

        def w_of(e):
            w = w_ex[e].rearrange("p (s k d) -> p s k d", s=3, k=2)
            return w[:, 0], w[:, 1], w[:, 2].rearrange("p k (m d) -> p k m d", m=MT)

        def blocks(eng, block_of):
            block_of(eng, 0)
            with eng.Fori(1, NB) as b:
                block_of(eng, b)

        def up(pe, b, e):
            n = EX * b + e
            if e < NE:
                wait(pe, m["c_read"], NE * b + e)
                pe.matmul(c_bank[:, :], sel[0:KC, e, :], cT[0:KC, :], start=True, stop=True).then_inc(m["c_bcast"], 1)
            hi, lo = xT_hi[:, bass.ds(b * L, L)], xT_lo[:, bass.ds(b * L, L)]
            wg, wu, _ = w_of(e)
            for k in range(MT):
                c = slice(k * P, (k + 1) * P)
                wait(pe, m["silu"], MT * n + k - 1 if e else MT * n)
                split3(pe, g_bank[k], wg[:, 0, c], wg[:, 1, c], hi, lo).then_inc(m["g_done"], 1)
                wait(pe, m["h_done"], MT * n + k - 1 if e else MT * n)
                split3(pe, u_bank[k], wu[:, 0, c], wu[:, 1, c], hi, lo).then_inc(m["u_done"], 1)

        def down(pe, b, e):
            n = EX * b + e
            if e == 0:
                wait(pe, m["y_read"], b)
            wait(pe, m["h_lo"], MT * n + MT)
            wd = w_of(e)[2]
            hs = h_sp[:, e % 2]
            for k in range(MT):
                first, final = e == 0 and k == 0, e == EX - 1 and k == MT - 1
                pe.matmul(y_bank[:, :], wd[:, 0, k], hs[:, 0, k], start=first, stop=False)
                pe.matmul(y_bank[:, :], wd[:, 0, k], hs[:, 1, k], start=False, stop=False)
                last = pe.matmul(y_bank[:, :], wd[:, 1, k], hs[:, 0, k], start=False, stop=final)
            last.then_inc(m["down_done"], 1)

        with nc.Block() as block:
            @block.tensor
            def _(pe):
                def block_of(pe, b):
                    wait(pe, m["c_copied"], b + 1)
                    wait(pe, m["out_done"], b)
                    for t in range(KT):
                        last = pe.transpose(t_bank[0:NE, t * P:(t + 1) * P], c4[:, t, :], ident[:, :])
                    last.then_inc(m["c_transposed"], 1)
                    wait(pe, m["c_lo"], b + 1)
                    for e in range(EX):
                        up(pe, b, e)
                        if e >= 1:
                            down(pe, b, e - 1)
                    down(pe, b, EX - 1)
                    wait(pe, m["y_read"], b + 1)
                    for t in range(KT):
                        last = pe.transpose(t_bank[:, t * P:(t + 1) * P], y_sb[:, t * P:(t + 1) * P], ident[:, :])
                    last.then_inc(m["yt_done"], 1)

                blocks(pe, block_of)

            @block.scalar
            def _(act):
                def high(b, e, k):
                    n = EX * b + e
                    wait(act, m["h_done"], MT * n + k + 1)
                    wait(act, m["down_done"], n - 1 if e else n)
                    act.activation(h_sp[:, e % 2, 0, k], hf[:, k], ACT.Copy).then_inc(m["h_hi"], 1)

                def block_of(act, b):
                    wait(act, m["c_transposed"], b + 1)
                    wait(act, m["c_bcast"], NE * b)
                    act.activation(cT[0:NE, :], t_bank[0:NE, :], ACT.Copy).then_inc(m["c_hi"], 1)
                    for e in range(EX):
                        n = EX * b + e
                        if e < NE:
                            wait(act, m["c_bcast"], NE * b + e + 1)
                            if e >= 2:
                                wait(act, m["sc_done"], MT * (NE * b + e - 1))
                            else:
                                wait(act, m["sc_done"], MT * NE * b)
                            act.activation(cb[:, e % 2], c_bank[:, :], ACT.Copy).then_inc(m["c_read"], 1)
                        for k in range(MT):
                            wait(act, m["g_done"], MT * n + k + 1)
                            if e >= 1:
                                wait(act, m["sc_done"], MT * (NE * b + e - 1) + k + 1)
                            else:
                                wait(act, m["h_done"], MT * n)
                            act.activation(sl[:, k], g_bank[k], ACT.Silu).then_inc(m["silu"], 1)
                        if e >= 1:
                            for k in range(MT):
                                high(b, e - 1, k)
                    for k in range(MT):
                        high(b, EX - 1, k)
                    wait(act, m["down_done"], EX * (b + 1))
                    wait(act, m["yt_done"], b)
                    act.activation(y_sb, y_bank[:, :], ACT.Copy).then_inc(m["y_read"], 1)

                blocks(act, block_of)

            @block.gpsimd
            def _(pool):
                def block_of(pool, b):
                    for e in range(NE):
                        n = EX * b + e
                        wait(pool, m["c_read"], NE * b + e + 1)
                        for k in range(MT):
                            wait(pool, m["silu"], MT * n + k + 1)
                            if e >= 1:
                                wait(pool, m["h_done"], MT * (n - 1) + k + 1)
                            else:
                                wait(pool, m["h_done"], MT * n)
                            pool.tensor_tensor(sc[:, k], sl[:, k], cb[:, e % 2], ALU.mult).then_inc(m["sc_done"], 1)

                blocks(pool, block_of)

            @block.vector
            def _(dve):
                def low(b, e, k):
                    n = EX * b + e
                    wait(dve, m["h_hi"], MT * n + k + 1)
                    hs = h_sp[:, e % 2]
                    dve.tensor_tensor(hs[:, 1, k], hf[:, k], hs[:, 0, k].bitcast(fp32), ALU.subtract).then_inc(m["h_lo"], 1)

                def block_of(dve, b):
                    wait(dve, m["c_transposed"], b)
                    dve.tensor_copy(c4[:, :, :], cwk[:, bass.ds(KT * b, KT), :]).then_inc(m["c_copied"], 1)
                    wait(dve, m["c_hi"], b + 1)
                    dve.tensor_tensor(cT[32:32 + NE, :], t_bank[0:NE, :], cT[0:NE, :].bitcast(fp32),
                                      ALU.subtract).then_inc(m["c_lo"], 1)
                    for e in range(EX):
                        n = EX * b + e
                        for k in range(MT):
                            wait(dve, m["u_done"], MT * n + k + 1)
                            if e < NE:
                                wait(dve, m["sc_done"], MT * (NE * b + e) + k + 1)
                            else:
                                wait(dve, m["silu"], MT * n + k + 1)
                            wait(dve, m["h_lo"], MT * (n - 1) + k + 1 if e else MT * n)
                            src = sc if e < NE else sl
                            dve.tensor_tensor(hf[:, k], u_bank[k], src[:, k], ALU.mult).then_inc(m["h_done"], 1)
                        for k in range(MT):
                            low(b, e, k)
                    wait(dve, m["yt_done"], b + 1)
                    wait(dve, m["out_put"], 16 * b)
                    xs = x_res[:, bass.ds(KT * b, KT), :].rearrange("p t d -> p (t d)")
                    dve.tensor_tensor(o_out[:, 0], t_bank[:, :], xs, ALU.add).then_inc(m["out_done"], 1)

                blocks(dve, block_of)

            @block.sync
            def _(sp):
                def block_of(sp, b):
                    wait(sp, m["out_done"], b + 1)
                    sp.dma_start(out_tok[:, bass.ds(KT * b, KT), :],
                                 o_out[:, 0].rearrange("p (t d) -> p t d", d=D)).then_inc(m["out_put"], 16)

                blocks(sp, block_of)
                wait(sp, m["out_put"], 16 * NB)


_INS = ["L0_attn_data", "L0_attn_W_qkv", "L0_attn_b_qkv", "L0_attn_W_out", "L0_attn_b_out", "L0_ffn_gate_w",
        "L0_ffn_beta", "L0_ffn_gate_proj_w", "L0_ffn_up_proj_w", "L0_ffn_down_proj_w", "L0_ffn_shared_gate_w",
        "L0_ffn_shared_up_w", "L0_ffn_shared_down_w"]
_OUT = ((8, 512, 128), "float32")


def kernel(**inputs):
    import numpy as _np
    import concourse.bacc as _bacc
    from concourse import mybir as _mybir
    from concourse.bass_utils import run_bass_kernel_spmd as _run

    nc = _bacc.Bacc("TRN2", target_bir_lowering=False, num_devices=1)
    arrays, args = {}, []
    for name in _INS:
        a = _np.ascontiguousarray(inputs[name])
        arrays[f"in_{name}_dram"] = a
        args.append(nc.dram_tensor(f"in_{name}_dram", a.shape, _mybir.dt.from_np(a.dtype), kind="ExternalInput").ap())
    shape, dtype = _OUT
    args.append(nc.dram_tensor("out_dram", shape, _mybir.dt.from_np(_np.dtype(dtype)), kind="ExternalOutput").ap())
    preln_attention_moe_kernel(nc, *args)
    r = _run(nc, [arrays], core_ids=[0])
    return r.results[0]["out_dram"]
```

```python
import concourse.bass as bass
from concourse import mybir
from contextlib import ExitStack


def preln_attention_moe_kernel(
    nc, x_in, w_qkv, b_qkv, w_out, b_out, gate_w, beta, gate_proj, up_proj, down_proj,
    shared_gate, shared_up, shared_down, out,
):
    fp32, fp32r, fp16, u32 = mybir.dt.float32, mybir.dt.float32r, mybir.dt.float16, mybir.dt.uint32
    ALU, ACT, AX = mybir.AluOpType, mybir.ActivationFunctionType, mybir.AxisListType

    NB, L, D = x_in.shape
    P = 128
    T = NB * L
    NT = T // P
    HD = 64
    DIM = w_out.shape[0]
    NPAIR = DIM // (2 * HD)
    KT = L // P
    NE, M = gate_w.shape[0], gate_proj.shape[2]
    MT = M // P
    EX = NE + 1
    UNITS = NB * NPAIR
    EPS = 1e-5
    SCALE = float(HD) ** -0.5
    SHIFT = 32.0

    x_tok = x_in.rearrange("n (t p) d -> p (n t) d", p=P)
    out_tok = out.rearrange("n (t p) d -> p (n t) d", p=P)

    ctx = ExitStack()
    with ctx:
        def sb(name, shape, dt):
            return ctx.enter_context(nc.sbuf_tensor(name, shape, dt))

        def sem(name):
            return ctx.enter_context(nc.semaphore(name))

        def bank(name, cols=512):
            return ctx.enter_context(nc.psum_tensor(name, [P, cols], fp32))

        def wait(eng, s, n):
            if not isinstance(n, int) or n > 0:
                eng.wait_ge(s, n)

        x_res = sb("x_res", [P, NT, D], fp32)
        xT = sb("xT", [P, 2, T], fp32r)
        xT_hi, xT_lo = xT[:, 0], xT[:, 1]
        yT = sb("yT", [P, T], fp32)
        xn = yT[:, :].rearrange("p (t d) -> p t d", d=D)
        R1 = sb("R1", [P, 14336], fp32r)
        o = 0
        QK = 2 * 2 * L
        qk = R1[:, 0:4 * QK].rearrange("p (b h s q) -> p b h s q", b=2, h=2, s=4)
        q1, q2, k1, k2 = (qk[:, :, :, j] for j in range(4))
        o = 4 * QK
        wqk = R1[:, o:o + 4096].rearrange("p (r s d) -> p r s d", r=NPAIR, s=4)
        wv_hi = R1[:, o + 4096:o + 5120]
        wv_lo = R1[:, o + 5120:o + 6144]
        WEX = 2 * 2 * M + 2 * MT * D
        w_ex = [R1[:, e * WEX:(e + 1) * WEX] for e in range(EX)]
        cT = R1[:, EX * WEX:EX * WEX + L]
        wo = sb("wo", [P, NPAIR, 2, D], fp32r)
        R2 = sb("R2", [P, 4096], fp32r)
        nat = R2[:, 0:2048].rearrange("p (s q) -> p s q", s=4)
        oT = R2[:, 2048:3072].rearrange("p (s q) -> p s q", s=2)
        r_wqk = R2[:, 3072:4096].rearrange("p (b s d) -> p b s d", b=2, s=4)
        h_sp = R2[:, :].rearrange("p (b s m q) -> p b s m q", b=2, s=2, m=MT)
        r_x = sb("r_x", [P, 2, D], fp32r)
        r_wo = sb("r_wo", [P, 2, 2, D], fp32r)
        r_b = sb("r_b", [P, 2, 2], fp32)
        VD = 2 * HD + 1
        r_v = sb("r_v", [P, KT, 2, 2, VD], fp16)
        m_row = sb("m_row", [KT, 2, P], fp32r)
        e32 = x_res[:, 0:16, :].rearrange("p (a t) d -> p a (t d)", a=2)
        o_sb = x_res[:, 16:16 + KT, :]
        prob = sb("prob", [P, 2, 2, KT, L], fp16)
        VW = 2 * KT * 2 * NPAIR
        v_all = sb("v_all", [P, VW * VD], fp16)
        v_hl = v_all[:, :].rearrange("p (t h d) -> p t h d", t=2 * KT, d=VD)
        v32 = v_all[:, :].bitcast(fp32)
        sq = prob[:, :, :, :, :].rearrange("p a b c d -> p (a b c d)").bitcast(fp32)
        mx = sb("mx", [P, 2, KT], fp32)
        rec = sb("rec", [P, KT], fp32)
        ident = sb("ident", [P, P], fp32)
        bqk = sb("bqk", [P, NPAIR, 2], fp32)
        bv = sb("bv", [P, NPAIR], fp32)
        bo = sb("bo", [P, 1], fp32)
        wb = sb("wb", [P, 1], fp32)
        mu = sb("mu", [P, NT], fp32)
        var = sb("var", [P, NT], fp32)
        rstd = sb("rstd", [P, NT], fp32)
        gwT = sb("gwT", [P, NE], fp32)
        beta_b = sb("beta_b", [P, NE], fp32)

        banks = [bank(f"bank{i}") for i in range(2)]
        s_bank = [bank(f"scores{i}", 1024) for i in range(2)]
        o_bank, x_bank = bank("o_bank"), bank("x_bank")

        s_x = [sem(f"x_in{g}") for g in range(4)]
        s_wraw, s_bias, s_small = sem("w_raw"), sem("bias_in"), sem("small_in")
        s_cst, s_wsp = sem("constants"), sem("w_split")
        s_wb = sem("wb_done")
        s_ln, s_sq, s_std = sem("ln_step"), sem("squared"), sem("std")
        s_tr, s_xh, s_xl = sem("x_transposed"), sem("x_hi"), sem("x_lo")
        GT = NT // 4

        raw_w = v32[:, 0:3 * DIM]
        raw_wo = v32[:, 3 * DIM:3 * DIM + NPAIR * D].rearrange("p (r d) -> p r d", r=NPAIR)

        def layernorm(dve, base, first):
            n = base
            for g in range(4):
                a, b = g * GT, (g + 1) * GT
                if first:
                    dve.wait_ge(s_x[g], 16)
                bc = lambda t: t[:, a:b].unsqueeze(2).to_broadcast([P, GT, D])
                dve.reduce_sum(mu[:, a:b], x_res[:, a:b, :], AX.X).then_inc(s_ln, 1)
                n += 1
                dve.wait_ge(s_ln, n)
                dve.tensor_scalar(mu[:, a:b], mu[:, a:b], 1.0 / D, None, ALU.mult).then_inc(s_ln, 1)
                n += 1
                dve.wait_ge(s_ln, n)
                dve.tensor_tensor(xn[:, a:b, :], x_res[:, a:b, :], bc(mu), ALU.subtract).then_inc(s_ln, 1)
                n += 1
            for g in range(4):
                a, b = g * GT, (g + 1) * GT
                bc = lambda t: t[:, a:b].unsqueeze(2).to_broadcast([P, GT, D])
                dve.wait_ge(s_sq, (0 if first else 4) + g + 1)
                dve.reduce_sum(var[:, a:b], sq[:, a * D:b * D].rearrange("p (t d) -> p t d", d=D), AX.X).then_inc(s_ln, 1)
                n += 1
                dve.wait_ge(s_ln, n)
                dve.tensor_scalar(var[:, a:b], var[:, a:b], 1.0 / D, EPS, ALU.mult, ALU.add).then_inc(s_ln, 1)
                n += 1
                dve.wait_ge(s_std, (0 if first else 4) + g + 1)
                dve.reciprocal(rstd[:, a:b], var[:, a:b]).then_inc(s_ln, 1)
                n += 1
                dve.wait_ge(s_ln, n)
                dve.tensor_tensor(xn[:, a:b, :], xn[:, a:b, :], bc(rstd), ALU.mult).then_inc(s_ln, 1)
                n += 1
            return n

        LN_STEPS = 4 * 3 + 4 * 4

        def layernorm_act(act, base, first):
            for g in range(4):
                act.wait_ge(s_ln, base + 3 * (g + 1))
                act.activation(sq[:, g * GT * D:(g + 1) * GT * D],
                               yT[:, g * GT * D:(g + 1) * GT * D], ACT.Square).then_inc(s_sq, 1)
            for g in range(4):
                act.wait_ge(s_ln, base + 12 + 4 * g + 2)
                act.activation(var[:, g * GT:(g + 1) * GT], var[:, g * GT:(g + 1) * GT],
                               ACT.Sqrt).then_inc(s_std, 1)

        def transpose_pe(pe, base, done):
            for b in range(NB):
                pe.wait_ge(s_ln, base + 12 + 4 * (b // 2 + 1))
                if done + b >= 2:
                    pe.wait_ge(s_xl, done + b - 1)
                for t in range(KT):
                    last = pe.transpose(banks[b % 2][:, t * P:(t + 1) * P], xn[:, KT * b + t, :], ident[:, :])
                last.then_inc(s_tr, 1)

        def transpose_hi(act, done):
            for b in range(NB):
                act.wait_ge(s_tr, done + b + 1)
                act.activation(xT_hi[:, b * L:(b + 1) * L], banks[b % 2][:, :], ACT.Copy).then_inc(s_xh, 1)

        def transpose_lo(dve, done):
            for b in range(NB):
                dve.wait_ge(s_xh, done + b + 1)
                dve.tensor_tensor(xT_lo[:, b * L:(b + 1) * L], banks[b % 2][:, :],
                                  xT_hi[:, b * L:(b + 1) * L], ALU.subtract).then_inc(s_xl, 1)

        with nc.Block() as block:
            @block.sync
            def _(sp):
                for g in range(4):
                    sp.dma_start(x_res[:, g * GT:(g + 1) * GT, :], x_tok[:, g * GT:(g + 1) * GT, :]).then_inc(s_x[g], 16)
                sp.dma_start(raw_w, w_qkv).then_inc(s_wraw, 16)
                sp.dma_start(raw_wo, w_out.rearrange("(r p) d -> p r d", p=P)).then_inc(s_wraw, 16)
                with nc.allow_non_contiguous_dma(reason="biases by partition"):
                    for s in range(2):
                        sp.dma_start(bqk[:, :, s], b_qkv[s * DIM:(s + 1) * DIM].rearrange("(r p) -> p r", p=P)).then_inc(s_bias, 16)
                    sp.dma_start(bv[:, :], b_qkv[2 * DIM:].rearrange("(r p) -> p r", p=P)).then_inc(s_bias, 16)
                    sp.dma_start(bo[:, :], b_out.rearrange("(p o) -> p o", o=1)).then_inc(s_bias, 16)
                    sp.dma_start(gwT[:, :], gate_w.rearrange("e h -> h e")).then_inc(s_small, 16)
                    sp.dma_start(beta_b[:, :], beta.rearrange("(o e) -> o e", o=1).to_broadcast([P, NE])).then_inc(s_small, 16)

            @block.gpsimd
            def _(pool):
                pool.memset(ident[:, :], 0.0).then_inc(s_cst, 1)
                pool.wait_ge(s_cst, 1)
                pool.affine_select(out=ident[:, :], in_=ident[:, :], compare_op=ALU.not_equal, fill=1.0,
                                   base=0, pattern=[[-1, P]], channel_multiplier=1).then_inc(s_cst, 1)
                pool.wait_ge(s_wraw, 32)
                wq3 = raw_w.rearrange("p (s r d) -> p s r d", s=3, r=NPAIR)
                parts = [(wqk[:, :, 0, :], wqk[:, :, 1, :], wq3[:, 0]), (wqk[:, :, 2, :], wqk[:, :, 3, :], wq3[:, 1]),
                         (wv_hi.rearrange("p (r d) -> p r d", r=NPAIR), wv_lo.rearrange("p (r d) -> p r d", r=NPAIR), wq3[:, 2]),
                         (wo[:, :, 0, :], wo[:, :, 1, :], raw_wo)]
                for hi, lo, raw in parts:
                    pool.tensor_copy(hi, raw).then_inc(s_wsp, 1)
                for n, (hi, lo, raw) in enumerate(parts):
                    pool.wait_ge(s_wsp, n + 1)
                    pool.tensor_tensor(lo, raw, hi, ALU.subtract).then_inc(s_wsp, 1)

            @block.vector
            def _(dve):
                dve.memset(k2[HD:HD + 1].bitcast(fp32), 1.0).then_inc(s_wb, 1)
                layernorm(dve, 0, True)
                transpose_lo(dve, 0)
                dve.wait_ge(s_wb, 2)
                dve.wait_ge(s_bias, 64)
                dve.tensor_tensor(wb[:, :], x_bank[:, 0:1], bo[:, :], ALU.add).then_inc(s_cst, 1)

            @block.scalar
            def _(act):
                layernorm_act(act, 0, True)
                transpose_hi(act, 0)

            @block.tensor
            def _(pe):
                pe.wait_ge(s_cst, 2)
                transpose_pe(pe, 0, 0)
                pe.wait_ge(s_wraw, 32)
                pe.wait_ge(s_bias, 64)
                for r in range(NPAIR):
                    last = pe.matmul(x_bank[:, 0:1], raw_wo[:, r, :], bv[:, r:r + 1], start=(r == 0), stop=(r == NPAIR - 1))
                last.then_inc(s_wb, 1)

        names = ("q_done k_done v_done ot_done y_done mt_done max_mm s_mm pv_mm exp_done q_hi k_hi v_hi "
                 "o_hi mrow q_lo k_lo v_lo o_lo maxed o_norm o_rec y_acc p_lo put m_put0 m_put1 ld_wqk ld_wo ld_x ld_v y_init v_ones")
        S = {n: sem(n) for n in names.split()}
        s_q, s_k, s_v, s_ot, s_y, s_mt = (S[n] for n in ("q_done", "k_done", "v_done", "ot_done", "y_done", "mt_done"))
        s_mm, s_sm, s_pv = S["max_mm"], S["s_mm"], S["pv_mm"]
        s_exp, s_qh, s_kh, s_vh, s_oh, s_mr = (S[n] for n in ("exp_done", "q_hi", "k_hi", "v_hi", "o_hi", "mrow"))
        s_ql, s_kl, s_vl, s_ol, s_mx, s_on, s_rec, s_ya = (
            S[n] for n in ("q_lo", "k_lo", "v_lo", "o_lo", "maxed", "o_norm", "o_rec", "y_acc"))
        s_pl, s_put, s_mp = S["p_lo"], S["put"], (S["m_put0"], S["m_put1"])
        s_lw, s_lo, s_lx, s_lv = S["ld_wqk"], S["ld_wo"], S["ld_x"], S["ld_v"]
        s_yi, s_v1 = S["y_init"], S["v_ones"]
        CH = NPAIR
        PUT = 6 * 16

        def split3(pe, out_ap, sta_hi, sta_lo, mov_hi, mov_lo):
            pe.matmul(out_ap, sta_hi, mov_hi, start=True, stop=False)
            pe.matmul(out_ap, sta_hi, mov_lo, start=False, stop=False)
            return pe.matmul(out_ap, sta_lo, mov_hi, start=False, stop=True)

        def pe_q(pe, u, par, x_hi, x_lo):
            pe.wait_ge(s_lw, 32 * (u // 2 + 1))
            if not (isinstance(u, int) and u < 2):
                pe.wait_ge(s_mr, 2 * (u - 1))
            elif u:
                pe.wait_ge(s_kl, u)
            split3(pe, x_bank[:, :], r_wqk[:, par, 0], r_wqk[:, par, 1], x_hi, x_lo).then_inc(s_q, 1)

        def pe_k(pe, u, par, x_hi, x_lo):
            pe.wait_ge(s_ql, u + 1)
            split3(pe, x_bank[:, :], r_wqk[:, par, 2], r_wqk[:, par, 3], x_hi, x_lo).then_inc(s_k, 1)

        def pe_max(pe, u, par, h, ts):
            if h == 0 and ts[0] == 0:
                pe.wait_ge(s_put, PUT * (u + 1))
            for t in ts:
                g = 8 * u + 4 * h + t
                wait(pe, s_mx, g - 1)
                pe.matmul(banks[t % 2][:, :], q1[:, par, h, t * P:(t + 1) * P], k1[:, par, h, :],
                          start=True, stop=True).then_inc(s_mm, 1)

        def pe_mt(pe, u, h, before, n):
            wait(pe, before, n)
            pe.wait_ge(s_mx, 8 * u + 4 * h + 4)
            pe.transpose(x_bank[0:KT, 0:P], mx[:, h, :], ident[:, :]).then_inc(s_mt, 1)

        def pe_scores(pe, u, par, h, half):
            wait(pe, s_exp, 4 * u + 2 * h + half - 1)
            pe.wait_ge(s_mp[h], 16 * (u + 1))
            R = HD + 1
            for t in range(2):
                c = (2 * half + t) * P
                dst = s_bank[half][:, t * L:(t + 1) * L]
                pe.matmul(dst, k1[:, par, h, c:c + P], q1[:, par, h, :], start=True, stop=False)
                last = pe.matmul(dst, k2[0:R, par, h, c:c + P], q2[0:R, par, h, :], start=False, stop=True)
            last.then_inc(s_sm, 1)

        def pe_pv(pe, u, par, h, qs):
            if qs[0] == 0:
                pe.wait_ge(s_pl, 4 * u + 2 * h + 2)
                pe.wait_ge(s_lv, 16 * (u // 2 + 1))
                wait(pe, s_on, 2 * u + h)
            for q in qs:
                dst = o_bank[:, q * (HD + 1):(q + 1) * (HD + 1)]
                for t in range(KT):
                    hi = prob[:, 0, h, t, q * P:(q + 1) * P]
                    lo = prob[:, 1, h, t, q * P:(q + 1) * P]
                    v = r_v[:, t, par, h, :]
                    pe.matmul(dst, hi, v[:, 0:HD + 1], start=(t == 0), stop=False)
                    pe.matmul(dst[:, 0:HD], hi, v[:, HD + 1:], start=False, stop=False)
                    last = pe.matmul(dst, lo, v[:, 0:HD + 1], start=False, stop=(t == KT - 1))
            if qs[-1] == KT - 1:
                last.then_inc(s_pv, 1)

        def pe_ot(pe, u, before, n):
            wait(pe, before, n)
            pe.wait_ge(s_on, 2 * u + 2)
            for t in range(KT):
                last = pe.transpose(x_bank[:, t * P:(t + 1) * P], o_sb[:, t, :], ident[:, :])
            last.then_inc(s_ot, 1)

        def pe_y(pe, u, par):
            pe.wait_ge(s_ol, u + 1)
            pe.wait_ge(s_lo, 16 * (u // 2 + 1))
            split3(pe, x_bank[:, :], r_wo[:, par, 0], r_wo[:, par, 1], oT[:, 0], oT[:, 1]).then_inc(s_y, 1)

        def pe_v(pe, u, c, before, n):
            wait(pe, before, n)
            pe.wait_ge(s_lx, 16 * (u // 2 + 1))
            h = slice(c * L, (c + 1) * L)
            split3(pe, x_bank[:, :], r_x[:, 0], r_x[:, 1], wv_hi[:, h], wv_lo[:, h]).then_inc(s_v, 1)

        def x_of(u):
            n = u // NPAIR
            if isinstance(n, int):
                return xT_hi[:, n * L:(n + 1) * L], xT_lo[:, n * L:(n + 1) * L]
            return xT_hi[:, bass.ds(n * L, L)], xT_lo[:, bass.ds(n * L, L)]

        def pe_unit(pe, u, par, first=False, nxt=True, nxt2=True):
            pe_scores(pe, u, par, 0, 0)
            if not first:
                pe_pv(pe, u - 1, 1 - par, 1, (0, 1))
            if nxt2:
                pe_q(pe, u + 2, par, *x_of(u + 2))
            if not first:
                pe_pv(pe, u - 1, 1 - par, 1, (2, 3))
            pe_scores(pe, u, par, 0, 1)
            if nxt2:
                pe_k(pe, u + 2, par, *x_of(u + 2))
            if nxt:
                pe_max(pe, u + 1, 1 - par, 0, (0, 1))
            pe_scores(pe, u, par, 1, 0)
            if not first:
                pe_ot(pe, u - 1, *((s_kl, u + 3) if nxt2 else (s_mr, 2 * u + 2)))
            if nxt:
                pe_max(pe, u + 1, 1 - par, 0, (2, 3))
            pe_scores(pe, u, par, 1, 1)
            if not first:
                pe_y(pe, u - 1, 1 - par)
            if nxt:
                pe_max(pe, u + 1, 1 - par, 1, (0, 1))
            if nxt2:
                pe_v(pe, u, par, *((s_kl, u + 3) if first else (s_ya, u)))
            pe_pv(pe, u, par, 0, (0, 1))
            if nxt:
                pe_mt(pe, u + 1, 0, *((s_vl, CH + u + 1) if nxt2 else (s_ya, u)))
                pe_max(pe, u + 1, 1 - par, 1, (2, 3))
            pe_pv(pe, u, par, 0, (2, 3))
            if nxt:
                pe_mt(pe, u + 1, 1, s_mr, 2 * (u + 1) + 1)

        def act_exp(act, u, h, half):
            act.wait_ge(s_sm, 4 * u + 2 * h + half + 1)
            wait(act, s_pl, 4 * u + 2 * h + half - 1)
            if half == 0:
                wait(act, s_pv, 2 * u + h - 1)
            act.activation(e32[:, half, :], s_bank[half][:, :], ACT.Exp, scale=SCALE)
            dst = prob[:, 0, h, 2 * half:2 * half + 2, :].rearrange("p t q -> p (t q)")
            act.activation(dst, s_bank[half][:, :], ACT.Exp, scale=SCALE).then_inc(s_exp, 1)

        def act_hi(act, u, par, s, done, own):
            act.wait_ge(done, u + 1)
            if s == 0:
                wait(act, s_put, PUT * u)
            act.activation(nat[:, 2 * s], x_bank[:, :], ACT.Identity, bias=r_b[:, par, s:s + 1]).then_inc(own, 1)

        def act_oh(act, u):
            act.wait_ge(s_ot, u + 1)
            wait(act, s_y, u)
            act.activation(oT[:, 0], x_bank[:, :], ACT.Copy).then_inc(s_oh, 1)

        def v_slot(u, c, part):
            n = ((u // NPAIR + 1) % 2) * KT + (u % NPAIR) // 2
            part = slice(0, HD) if part == 0 else slice(HD + 1, VD)
            if isinstance(u, int):
                return v_hl[:, n, c * NPAIR:(c + 1) * NPAIR, part]
            return v_hl[:, bass.ds(n, 1), c * NPAIR:(c + 1) * NPAIR, part].rearrange("p o h d -> p (o h) d")

        x3 = x_bank[:, :].rearrange("p (h d) -> p h d", d=HD)

        def act_vh(act, u, c):
            act.wait_ge(s_v, CH + u + 1)
            wait(act, s_lv, 16 * (u // 2))
            act.activation(v_slot(u, c, 0), x3, ACT.Copy).then_inc(s_vh, 1)

        def act_mr(act, u, h):
            act.wait_ge(s_mt, 2 * u + h + 1)
            wait(act, s_mp[h], 16 * u)
            act.activation(m_row[:, h, :], x_bank[0:KT, 0:P], ACT.Copy, bias=SHIFT, scale=-1.0).then_inc(s_mr, 1)

        def act_unit(act, u, par, first=False, nxt=True, nxt2=True):
            act_exp(act, u, 0, 0)
            if nxt2:
                act_hi(act, u + 2, par, 0, s_q, s_qh)
            act_exp(act, u, 0, 1)
            if nxt2:
                act_hi(act, u + 2, par, 1, s_k, s_kh)
            act_exp(act, u, 1, 0)
            if not first:
                act_oh(act, u - 1)
            act_exp(act, u, 1, 1)
            if nxt2:
                act_vh(act, u, par)
            if nxt:
                act_mr(act, u + 1, 0)
                act_mr(act, u + 1, 1)

        def dve_lo(dve, u, par, s, hi_done, own):
            dve.wait_ge(hi_done, u + 1)
            dve.scalar_tensor_tensor(out=nat[:, 2 * s + 1], in0=x_bank[:, :], scalar=r_b[:, par, s:s + 1],
                                     in1=nat[:, 2 * s].bitcast(fp32), op0=ALU.add, op1=ALU.subtract).then_inc(own, 1)

        def dve_max(dve, u, h, ts):
            if ts[0] == 0:
                wait(dve, s_mt, 2 * u + h - 1)
            for t in ts:
                dve.wait_ge(s_mm, 8 * u + 4 * h + t + 1)
                dve.reduce_max(mx[:, h, t:t + 1], banks[t % 2][:, :], AX.X).then_inc(s_mx, 1)

        def dve_norm(dve, u, h):
            dve.wait_ge(s_pv, 2 * u + h + 1)
            wait(dve, s_on, 2 * u + h)
            o3 = o_bank[:, 0:KT * (HD + 1)].rearrange("p (q d) -> p q d", d=HD + 1)
            dve.reciprocal(rec[:, :].unsqueeze(2), o3[:, :, HD:HD + 1]).then_inc(s_rec, 1)
            dve.wait_ge(s_rec, 2 * u + h + 1)
            wait(dve, s_ot, u)
            dve.tensor_tensor(o_sb[:, :, h * HD:(h + 1) * HD], o3[:, :, 0:HD],
                              rec[:, :].unsqueeze(2).to_broadcast([P, KT, HD]), ALU.mult).then_inc(s_on, 1)

        def dve_ol(dve, u):
            dve.wait_ge(s_oh, u + 1)
            wait(dve, s_y, u)
            dve.tensor_tensor(oT[:, 1], x_bank[:, :], oT[:, 0].bitcast(fp32), ALU.subtract).then_inc(s_ol, 1)

        def dve_ya(dve, u):
            dve.wait_ge(s_y, u + 1)
            wait(dve, s_ya, u)
            n = u // NPAIR
            y = yT[:, n * L:(n + 1) * L] if isinstance(n, int) else yT[:, bass.ds(n * L, L)]
            dve.tensor_tensor(y, x_bank[:, :], y, ALU.add).then_inc(s_ya, 1)

        def dve_vl(dve, u, c):
            dve.wait_ge(s_vh, CH + u + 1)
            dve.tensor_tensor(v_slot(u, c, 1), x3, v_slot(u, c, 0), ALU.subtract).then_inc(s_vl, 1)

        def dve_unit(dve, u, par, first=False, nxt=True, nxt2=True):
            if nxt2:
                dve_lo(dve, u + 2, par, 0, s_qh, s_ql)
            if not first:
                dve_norm(dve, u - 1, 1)
            if nxt2:
                dve_lo(dve, u + 2, par, 1, s_kh, s_kl)
            if nxt:
                dve_max(dve, u + 1, 0, (0, 1))
            if not first:
                dve_ol(dve, u - 1)
            if nxt:
                dve_max(dve, u + 1, 0, (2, 3))
            if not first:
                dve_ya(dve, u - 1)
            if nxt:
                dve_max(dve, u + 1, 1, (0, 1))
            if nxt2:
                dve_vl(dve, u, par)
            if nxt:
                dve_max(dve, u + 1, 1, (2, 3))
            dve_norm(dve, u, 0)

        def pool_unit(pool, u, par, first=False, nxt=True, nxt2=True):
            for h in range(2):
                for half in range(2):
                    pool.wait_ge(s_exp, 4 * u + 2 * h + half + 1)
                    if half == 0:
                        wait(pool, s_pv, 2 * u + h - 1)
                    view = lambda s: prob[:, s, h, 2 * half:2 * half + 2, :].rearrange("p t q -> p (t q)")
                    pool.tensor_tensor(view(1), e32[:, half, :], view(0), ALU.subtract).then_inc(s_pl, 1)

        def move(eng, dst, src):
            if src.dtype == fp32r:
                dst, src = dst.bitcast(fp32), src.bitcast(fp32)
            return eng.dma_start(dst, src)

        def put(sp, u, par):
            sp.wait_ge(s_kl, u + 1)
            if not (isinstance(u, int) and u < 2):
                sp.wait_ge(s_sm, 4 * (u - 1))
            A, B = slice(0, HD), slice(HD, P)
            for h, src in ((0, A), (1, B)):
                move(sp, qk[A, par, h, 0:3], nat[src, 0:3]).then_inc(s_put, 16)
                move(sp, qk[B, par, h, 0:4:2], nat[src, 0:4:3]).then_inc(s_put, 16)
                move(sp, k2[A, par, h], nat[src, 2]).then_inc(s_put, 16)

        def put_m(sp, u, par, h):
            sp.wait_ge(s_mr, 2 * u + h + 1)
            move(sp, q2[HD:HD + 1, par, h, :], m_row[:, h, :]).then_inc(s_mp[h], 16)

        def two(t, n):
            return t[:, n:n + 2] if isinstance(n, int) else t[:, bass.ds(n, 2)]

        def ld_wqk(sp, u):
            wait(sp, s_kl, u)
            move(sp, r_wqk, two(wqk, u % NPAIR)).then_inc(s_lw, 16)
            move(sp, r_b[:, :, :], two(bqk, u % NPAIR)).then_inc(s_lw, 16)

        def ld_wo(sp, u):
            wait(sp, s_y, u)
            move(sp, r_wo[:, :, :, :], two(wo, u % NPAIR)).then_inc(s_lo, 16)

        def ld_x(sp, u):
            wait(sp, s_v, CH + u)
            t = ((u // NPAIR + 1) % NB) * KT + (u % NPAIR) // 2
            src = xT[:, :, t * P:(t + 1) * P] if isinstance(t, int) else xT[:, :, bass.ds(t * P, P)]
            move(sp, r_x[:, :, :], src).then_inc(s_lx, 16)

        def ld_v(sp, u):
            if isinstance(u, int) and u == 0:
                sp.wait_ge(s_vl, CH)
            wait(sp, s_pv, 2 * u)
            n, r = u // NPAIR, u % NPAIR
            src = v_all[:, :].rearrange("p (b t r w) -> p b r t w", b=2, t=KT, r=NPAIR // 2)
            dst = r_v[:, :, :, :, :].rearrange("p t r h d -> p t (r h d)")
            if isinstance(u, int):
                src = src[:, n % 2, r // 2]
            else:
                src = src[:, bass.ds(n % 2, 1), bass.ds(r // 2, 1)].rearrange("p a b t w -> p (a b t) w")
            move(sp, dst, src).then_inc(s_lv, 16)

        def sp_unit(sp, u, par, first=False, nxt=True, nxt2=True):
            if par == 0:
                ld_v(sp, u)
            if par == 0:
                ld_wo(sp, u)
            if nxt2:
                put(sp, u + 2, par)
                if par == 1:
                    ld_wqk(sp, u + 3)
            if nxt:
                put_m(sp, u + 1, 1 - par, 0)
                put_m(sp, u + 1, 1 - par, 1)
            if par == 1 and nxt2:
                ld_x(sp, u + 1)

        def run_units(eng, step):
            step(eng, 0, 0, first=True)
            step(eng, 1, 1)
            with eng.Fori(1, UNITS // 2 - 1) as i:
                step(eng, 2 * i, 0)
                step(eng, 2 * i + 1, 1)
            step(eng, UNITS - 2, 0, nxt2=False)
            step(eng, UNITS - 1, 1, nxt=False, nxt2=False)

        with nc.Block() as block:
            @block.sync
            def _(sp):
                sp.wait_ge(s_v1, 1)
                ld_wqk(sp, 0)
                put(sp, 0, 0)
                put(sp, 1, 1)
                ld_wqk(sp, 2)
                ld_x(sp, 0)
                put_m(sp, 0, 0, 0)
                put_m(sp, 0, 0, 1)
                run_units(sp, sp_unit)
                sp.wait_ge(s_lw, 32 * (UNITS // 2 + 1))
                sp.wait_ge(s_lx, 16 * UNITS // 2)

            @block.gpsimd
            def _(pool):
                pool.memset(yT[:, :], 0.0).then_inc(s_yi, 1)
                pool.memset(v_hl[:, :, :, HD:HD + 1], 1.0).then_inc(s_v1, 1)
                run_units(pool, pool_unit)

            @block.scalar
            def _(act):
                for u in range(2):
                    act_hi(act, u, u, 0, s_q, s_qh)
                    act_hi(act, u, u, 1, s_k, s_kh)
                for c in range(CH):
                    act.wait_ge(s_v, c + 1)
                    act.activation(v_hl[:, c // 2, (c % 2) * NPAIR:(c % 2 + 1) * NPAIR, 0:HD],
                                   s_bank[c % 2][:, 0:L].rearrange("p (h d) -> p h d", d=HD), ACT.Copy).then_inc(s_vh, 1)
                act_mr(act, 0, 0)
                act_mr(act, 0, 1)
                run_units(act, act_unit)
                act_oh(act, UNITS - 1)

            @block.vector
            def _(dve):
                for u in range(2):
                    dve_lo(dve, u, u, 0, s_qh, s_ql)
                    dve_lo(dve, u, u, 1, s_kh, s_kl)
                for c in range(CH):
                    dve.wait_ge(s_vh, c + 1)
                    h = slice((c % 2) * NPAIR, (c % 2 + 1) * NPAIR)
                    dve.tensor_tensor(v_hl[:, c // 2, h, HD + 1:], s_bank[c % 2][:, 0:L].rearrange("p (h d) -> p h d", d=HD),
                                      v_hl[:, c // 2, h, 0:HD], ALU.subtract).then_inc(s_vl, 1)
                dve_max(dve, 0, 0, range(KT))
                dve_max(dve, 0, 1, range(KT))
                dve.wait_ge(s_yi, 1)
                dve.tensor_scalar(yT[:, :], yT[:, :], wb[:, 0:1], None, ALU.add).then_inc(s_yi, 1)
                dve.wait_ge(s_yi, 2)
                run_units(dve, dve_unit)
                dve_norm(dve, UNITS - 1, 1)
                dve_ol(dve, UNITS - 1)
                dve_ya(dve, UNITS - 1)

            @block.tensor
            def _(pe):
                for u in range(2):
                    pe_q(pe, u, u, *x_of(u))
                    pe_k(pe, u, u, *x_of(u))
                for c in range(CH):
                    if c >= 2:
                        pe.wait_ge(s_vl, c - 1)
                    t = slice((c // 2) * P, (c // 2 + 1) * P)
                    h = slice((c % 2) * L, (c % 2 + 1) * L)
                    split3(pe, s_bank[c % 2][:, 0:L], xT_hi[:, t], xT_lo[:, t], wv_hi[:, h], wv_lo[:, h]).then_inc(s_v, 1)
                pe.wait_ge(s_vl, CH)
                pe_max(pe, 0, 0, 0, range(KT))
                pe_max(pe, 0, 0, 1, range(KT))
                pe_mt(pe, 0, 0, s_kl, 2)
                pe_mt(pe, 0, 1, s_mr, 1)
                run_units(pe, pe_unit)
                pe_pv(pe, UNITS - 1, 1, 1, range(KT))
                pe_ot(pe, UNITS - 1, s_ya, UNITS - 1)
                pe_y(pe, UNITS - 1, 1)

        s_yt, s_xr = sem("y_transposed"), sem("x_residual")
        s_lgT, s_lg8, s_lt, s_lg = sem("logitsT"), sem("logitsT_read"), sem("logits_transposed"), sem("logits_read")
        s_gws, s_rt, s_sg, s_wx, s_wxs, s_sel = (
            sem("gate_split"), sem("route_step"), sem("route_exp"), sem("expert_raw"), sem("expert_split"), sem("select"))
        RAW = 3 * M
        gsp = wo[:, 0:1, :, :].rearrange("p o s d -> p (o s) d")
        sel = wo[:, 1:5, :, :].rearrange("p r s d -> p (r s) d")
        lgT = sq[0:NE, 3072:3072 + L]
        small = sq[:, 1024:3072]
        N8 = NT * NE
        lg, zb, mask, tmp, sig, cw = (small[:, j * N8:(j + 1) * N8].rearrange("p (t e) -> p t e", e=NE) for j in range(6))
        top = small[:, 6 * N8:7 * N8].rearrange("p (t e) -> p t e", e=NE)
        idx = small[:, 7 * N8:8 * N8].bitcast(u32).rearrange("p (t e) -> p t e", e=NE)
        cwk = zb
        c4 = sb("c4", [P, KT, NE], fp32)
        iota8 = sb("iota8", [P, NE], fp32)
        selw = sq[:, 0:NE * P].rearrange("p (e m) -> p e m", e=NE)

        with nc.Block() as block:
            @block.sync
            def _(sp):
                for g in range(4):
                    sp.dma_start(x_res[:, g * GT:(g + 1) * GT, :], x_tok[:, g * GT:(g + 1) * GT, :]).then_inc(s_x[g], 16)
                for e in range(EX):
                    g, u_, d_ = ((gate_proj[e], up_proj[e], down_proj[e]) if e < NE
                                 else (shared_gate[0], shared_up[0], shared_down[0]))
                    r = v32[:, e * RAW:(e + 1) * RAW]
                    sp.dma_start(r[:, 0:M], g).then_inc(s_wx, 16)
                    sp.dma_start(r[:, M:2 * M], u_).then_inc(s_wx, 16)
                    sp.dma_start(r[:, 2 * M:3 * M].rearrange("p (m d) -> p m d", m=MT),
                                 d_.rearrange("(m p) d -> p m d", p=P)).then_inc(s_wx, 16)

            @block.gpsimd
            def _(pool):
                pool.memset(gsp.rearrange("p s d -> p (s d)").bitcast(fp32), 0.0).then_inc(s_gws, 1)
                pool.wait_ge(s_gws, 1)
                pool.wait_ge(s_small, 32)
                pool.tensor_copy(gsp[:, 0, 0:NE], gwT[:, :]).then_inc(s_gws, 1)
                pool.wait_ge(s_gws, 2)
                pool.tensor_tensor(gsp[:, 1, 0:NE], gwT[:, :], gsp[:, 0, 0:NE].bitcast(fp32), ALU.subtract).then_inc(s_gws, 1)
                pool.iota(iota8[:, :], pattern=[[1, NE]], base=0, channel_multiplier=0,
                          allow_small_or_imprecise_dtypes=True).then_inc(s_gws, 1)
                pool.wait_ge(s_wx, 48 * EX)
                for e in range(EX):
                    raw = v32[:, e * RAW:(e + 1) * RAW].rearrange("p (s d) -> p s d", s=3)
                    w = w_ex[e].rearrange("p (s k d) -> p s k d", s=3, k=2)
                    pool.tensor_copy(w[:, :, 0, :], raw).then_inc(s_wxs, 1)
                    pool.wait_ge(s_wxs, 2 * e + 1)
                    pool.tensor_tensor(w[:, :, 1, :], raw, w[:, :, 0, :].bitcast(fp32), ALU.subtract).then_inc(s_wxs, 1)
                pool.memset(cT.bitcast(fp32), 0.0).then_inc(s_sel, 1)
                pool.wait_ge(s_ln, 2 * LN_STEPS)
                pool.memset(selw, 0.0).then_inc(s_sel, 1)
                for n, base in enumerate((0, -32)):
                    pool.wait_ge(s_sel, 2 + n)
                    pool.affine_select(out=selw, in_=selw, compare_op=ALU.not_equal, fill=1.0, base=base,
                                       pattern=[[-1, NE], [0, P]], channel_multiplier=1).then_inc(s_sel, 1)
                pool.wait_ge(s_sel, 4)
                pool.tensor_copy(sel, selw).then_inc(s_sel, 1)

            @block.vector
            def _(dve):
                for b in range(NB):
                    dve.wait_ge(s_yt, b + 1)
                    dve.wait_ge(s_x[b // 2], 32)
                    xs = x_res[:, KT * b:KT * (b + 1), :].rearrange("p t d -> p (t d)")
                    dve.tensor_tensor(xs, banks[b % 2][:, :], xs, ALU.add).then_inc(s_xr, 1)
                dve.wait_ge(s_xr, NB)
                layernorm(dve, LN_STEPS, False)
                transpose_lo(dve, NB)
                for b in range(NB):
                    dve.wait_ge(s_lgT, b + 1)
                    wait(dve, s_lt, b)
                    dve.tensor_copy(lgT, o_bank[0:NE, :]).then_inc(s_lg8, 1)
                    dve.wait_ge(s_lt, b + 1)
                    dve.tensor_copy(lg[:, KT * b:KT * (b + 1), :],
                                    x_bank[:, 0:KT * NE].rearrange("p (t e) -> p t e", e=NE)).then_inc(s_lg, 1)
                n = [0]

                def step(ins):
                    ins.then_inc(s_rt, 1)
                    n[0] += 1
                    dve.wait_ge(s_rt, n[0])

                dve.wait_ge(s_lg, NB)
                dve.wait_ge(s_small, 32)
                step(dve.tensor_tensor(zb, lg, beta_b[:, :].unsqueeze(1).to_broadcast([P, NT, NE]), ALU.add))
                for t in range(NT):
                    last = dve.max(top[:, t, :], zb[:, t, :])
                step(last)
                for t in range(NT):
                    last = dve.max_index(idx[:, t, :], top[:, t, :], zb[:, t, :])
                step(last)
                step(dve.tensor_copy(tmp, idx))
                dve.wait_ge(s_gws, 4)
                io = iota8[:, :].unsqueeze(1).to_broadcast([P, NT, NE])
                step(dve.tensor_tensor(mask, io, tmp[:, :, 0:1].to_broadcast([P, NT, NE]), ALU.is_equal))
                step(dve.tensor_tensor(top, io, tmp[:, :, 1:2].to_broadcast([P, NT, NE]), ALU.is_equal))
                step(dve.tensor_tensor(mask, mask, top, ALU.add))
                dve.wait_ge(s_sg, 1)
                step(dve.tensor_scalar(sig, sig, 1.0, None, ALU.add))
                step(dve.reciprocal(cw, sig))
                step(dve.tensor_tensor(cwk, cw, mask, ALU.mult))

            @block.scalar
            def _(act):
                layernorm_act(act, LN_STEPS, False)
                transpose_hi(act, NB)
                act.wait_ge(s_lg, NB)
                act.activation(sig, lg, ACT.Exp, scale=-1.0).then_inc(s_sg, 1)

            @block.tensor
            def _(pe):
                for b in range(NB):
                    if b >= 2:
                        pe.wait_ge(s_xr, b - 1)
                    for t in range(KT):
                        c = b * L + t * P
                        last = pe.transpose(banks[b % 2][:, t * P:(t + 1) * P], yT[:, c:c + P], ident[:, :])
                    last.then_inc(s_yt, 1)
                pe.wait_ge(s_xr, NB)
                transpose_pe(pe, LN_STEPS, NB)
                pe.wait_ge(s_gws, 3)
                for b in range(NB):
                    pe.wait_ge(s_xl, NB + b + 1)
                    wait(pe, s_lg8, b)
                    hi, lo = xT_hi[:, b * L:(b + 1) * L], xT_lo[:, b * L:(b + 1) * L]
                    pe.matmul(o_bank[:, :], gsp[:, 0], hi, start=True, stop=False)
                    pe.matmul(o_bank[:, :], gsp[:, 0], lo, start=False, stop=False)
                    pe.matmul(o_bank[:, :], gsp[:, 1], lo, start=False, stop=False)
                    pe.matmul(o_bank[:, :], gsp[:, 1], hi, start=False, stop=True).then_inc(s_lgT, 1)
                    pe.wait_ge(s_lg8, b + 1)
                    wait(pe, s_lg, b)
                    for t in range(KT):
                        last = pe.transpose(x_bank[:, t * NE:(t + 1) * NE], lgT[:, t * P:(t + 1) * P], ident[0:NE, 0:NE])
                    last.then_inc(s_lt, 1)

        names = ("c_copied c_transposed c_hi c_lo c_bcast c_read g_done u_done silu sc_done h_done h_hi h_lo "
                 "down_done y_read yt_done out_done out_put")
        S = {n: sem("m_" + n) for n in names.split()}
        m = S
        sl = yT[:, 0:2 * L].rearrange("p (m q) -> p m q", m=MT)
        sc = yT[:, 2 * L:4 * L].rearrange("p (m q) -> p m q", m=MT)
        hf = yT[:, 4 * L:6 * L].rearrange("p (m q) -> p m q", m=MT)
        cb = yT[:, 6 * L:8 * L].rearrange("p (b q) -> p b q", b=2)
        y_sb = sq[:, 2048:2048 + L]
        o_out = sq[:, 2560:2560 + 2 * L].rearrange("p (b q) -> p b q", b=2)
        g_bank = [s_bank[0][:, 0:L], s_bank[0][:, L:2 * L]]
        u_bank = [s_bank[1][:, 0:L], s_bank[1][:, L:2 * L]]
        c_bank, y_bank, t_bank = banks[0], banks[1], o_bank
        KC = 40

        def w_of(e):
            w = w_ex[e].rearrange("p (s k d) -> p s k d", s=3, k=2)
            return w[:, 0], w[:, 1], w[:, 2].rearrange("p k (m d) -> p k m d", m=MT)

        def blocks(eng, block_of):
            block_of(eng, 0)
            with eng.Fori(1, NB) as b:
                block_of(eng, b)

        def up(pe, b, e):
            n = EX * b + e
            if e < NE:
                wait(pe, m["c_read"], NE * b + e)
                pe.matmul(c_bank[:, :], sel[0:KC, e, :], cT[0:KC, :], start=True, stop=True).then_inc(m["c_bcast"], 1)
            hi, lo = xT_hi[:, bass.ds(b * L, L)], xT_lo[:, bass.ds(b * L, L)]
            wg, wu, _ = w_of(e)
            for k in range(MT):
                c = slice(k * P, (k + 1) * P)
                wait(pe, m["silu"], MT * n + k - 1 if e else MT * n)
                split3(pe, g_bank[k], wg[:, 0, c], wg[:, 1, c], hi, lo).then_inc(m["g_done"], 1)
                wait(pe, m["h_done"], MT * n + k - 1 if e else MT * n)
                split3(pe, u_bank[k], wu[:, 0, c], wu[:, 1, c], hi, lo).then_inc(m["u_done"], 1)

        def down(pe, b, e):
            n = EX * b + e
            if e == 0:
                wait(pe, m["y_read"], b)
            wait(pe, m["h_lo"], MT * n + MT)
            wd = w_of(e)[2]
            hs = h_sp[:, e % 2]
            for k in range(MT):
                first, final = e == 0 and k == 0, e == EX - 1 and k == MT - 1
                pe.matmul(y_bank[:, :], wd[:, 0, k], hs[:, 0, k], start=first, stop=False)
                pe.matmul(y_bank[:, :], wd[:, 0, k], hs[:, 1, k], start=False, stop=False)
                last = pe.matmul(y_bank[:, :], wd[:, 1, k], hs[:, 0, k], start=False, stop=final)
            last.then_inc(m["down_done"], 1)

        with nc.Block() as block:
            @block.tensor
            def _(pe):
                def block_of(pe, b):
                    wait(pe, m["c_copied"], b + 1)
                    wait(pe, m["out_done"], b)
                    for t in range(KT):
                        last = pe.transpose(t_bank[0:NE, t * P:(t + 1) * P], c4[:, t, :], ident[:, :])
                    last.then_inc(m["c_transposed"], 1)
                    wait(pe, m["c_lo"], b + 1)
                    for e in range(EX):
                        up(pe, b, e)
                        if e >= 1:
                            down(pe, b, e - 1)
                    down(pe, b, EX - 1)
                    wait(pe, m["y_read"], b + 1)
                    for t in range(KT):
                        last = pe.transpose(t_bank[:, t * P:(t + 1) * P], y_sb[:, t * P:(t + 1) * P], ident[:, :])
                    last.then_inc(m["yt_done"], 1)

                blocks(pe, block_of)

            @block.scalar
            def _(act):
                def high(b, e, k):
                    n = EX * b + e
                    wait(act, m["h_done"], MT * n + k + 1)
                    wait(act, m["down_done"], n - 1 if e else n)
                    act.activation(h_sp[:, e % 2, 0, k], hf[:, k], ACT.Copy).then_inc(m["h_hi"], 1)

                def block_of(act, b):
                    wait(act, m["c_transposed"], b + 1)
                    wait(act, m["c_bcast"], NE * b)
                    act.activation(cT[0:NE, :], t_bank[0:NE, :], ACT.Copy).then_inc(m["c_hi"], 1)
                    for e in range(EX):
                        n = EX * b + e
                        if e < NE:
                            wait(act, m["c_bcast"], NE * b + e + 1)
                            if e >= 2:
                                wait(act, m["sc_done"], MT * (NE * b + e - 1))
                            else:
                                wait(act, m["sc_done"], MT * NE * b)
                            act.activation(cb[:, e % 2], c_bank[:, :], ACT.Copy).then_inc(m["c_read"], 1)
                        for k in range(MT):
                            wait(act, m["g_done"], MT * n + k + 1)
                            if e >= 1:
                                wait(act, m["sc_done"], MT * (NE * b + e - 1) + k + 1)
                            else:
                                wait(act, m["h_done"], MT * n)
                            act.activation(sl[:, k], g_bank[k], ACT.Silu).then_inc(m["silu"], 1)
                        if e >= 1:
                            for k in range(MT):
                                high(b, e - 1, k)
                    for k in range(MT):
                        high(b, EX - 1, k)
                    wait(act, m["down_done"], EX * (b + 1))
                    wait(act, m["yt_done"], b)
                    act.activation(y_sb, y_bank[:, :], ACT.Copy).then_inc(m["y_read"], 1)

                blocks(act, block_of)

            @block.gpsimd
            def _(pool):
                def block_of(pool, b):
                    for e in range(NE):
                        n = EX * b + e
                        wait(pool, m["c_read"], NE * b + e + 1)
                        for k in range(MT):
                            wait(pool, m["silu"], MT * n + k + 1)
                            if e >= 1:
                                wait(pool, m["h_done"], MT * (n - 1) + k + 1)
                            else:
                                wait(pool, m["h_done"], MT * n)
                            pool.tensor_tensor(sc[:, k], sl[:, k], cb[:, e % 2], ALU.mult).then_inc(m["sc_done"], 1)

                blocks(pool, block_of)

            @block.vector
            def _(dve):
                def low(b, e, k):
                    n = EX * b + e
                    wait(dve, m["h_hi"], MT * n + k + 1)
                    hs = h_sp[:, e % 2]
                    dve.tensor_tensor(hs[:, 1, k], hf[:, k], hs[:, 0, k].bitcast(fp32), ALU.subtract).then_inc(m["h_lo"], 1)

                def block_of(dve, b):
                    wait(dve, m["c_transposed"], b)
                    dve.tensor_copy(c4[:, :, :], cwk[:, bass.ds(KT * b, KT), :]).then_inc(m["c_copied"], 1)
                    wait(dve, m["c_hi"], b + 1)
                    dve.tensor_tensor(cT[32:32 + NE, :], t_bank[0:NE, :], cT[0:NE, :].bitcast(fp32),
                                      ALU.subtract).then_inc(m["c_lo"], 1)
                    for e in range(EX):
                        n = EX * b + e
                        for k in range(MT):
                            wait(dve, m["u_done"], MT * n + k + 1)
                            if e < NE:
                                wait(dve, m["sc_done"], MT * (NE * b + e) + k + 1)
                            else:
                                wait(dve, m["silu"], MT * n + k + 1)
                            wait(dve, m["h_lo"], MT * (n - 1) + k + 1 if e else MT * n)
                            src = sc if e < NE else sl
                            dve.tensor_tensor(hf[:, k], u_bank[k], src[:, k], ALU.mult).then_inc(m["h_done"], 1)
                        for k in range(MT):
                            low(b, e, k)
                    wait(dve, m["yt_done"], b + 1)
                    wait(dve, m["out_put"], 16 * b)
                    xs = x_res[:, bass.ds(KT * b, KT), :].rearrange("p t d -> p (t d)")
                    dve.tensor_tensor(o_out[:, 0], t_bank[:, :], xs, ALU.add).then_inc(m["out_done"], 1)

                blocks(dve, block_of)

            @block.sync
            def _(sp):
                def block_of(sp, b):
                    wait(sp, m["out_done"], b + 1)
                    sp.dma_start(out_tok[:, bass.ds(KT * b, KT), :],
                                 o_out[:, 0].rearrange("p (t d) -> p t d", d=D)).then_inc(m["out_put"], 16)

                blocks(sp, block_of)
                wait(sp, m["out_put"], 16 * NB)


_INS = ["L0_attn_data", "L0_attn_W_qkv", "L0_attn_b_qkv", "L0_attn_W_out", "L0_attn_b_out", "L0_ffn_gate_w",
        "L0_ffn_beta", "L0_ffn_gate_proj_w", "L0_ffn_up_proj_w", "L0_ffn_down_proj_w", "L0_ffn_shared_gate_w",
        "L0_ffn_shared_up_w", "L0_ffn_shared_down_w"]
_OUT = ((8, 512, 128), "float32")


def kernel(**inputs):
    import numpy as _np
    import concourse.bacc as _bacc
    from concourse import mybir as _mybir
    from concourse.bass_utils import run_bass_kernel_spmd as _run

    nc = _bacc.Bacc("TRN2", target_bir_lowering=False, num_devices=1)
    arrays, args = {}, []
    for name in _INS:
        a = _np.ascontiguousarray(inputs[name])
        arrays[f"in_{name}_dram"] = a
        args.append(nc.dram_tensor(f"in_{name}_dram", a.shape, _mybir.dt.from_np(a.dtype), kind="ExternalInput").ap())
    shape, dtype = _OUT
    args.append(nc.dram_tensor("out_dram", shape, _mybir.dt.from_np(_np.dtype(dtype)), kind="ExternalOutput").ap())
    preln_attention_moe_kernel(nc, *args)
    r = _run(nc, [arrays], core_ids=[0])
    return r.results[0]["out_dram"]
```

```python
import concourse.bass as bass
from concourse import mybir
from contextlib import ExitStack


def preln_attention_moe_kernel(
    nc, x_in, w_qkv, b_qkv, w_out, b_out, gate_w, beta, gate_proj, up_proj, down_proj,
    shared_gate, shared_up, shared_down, out,
):
    fp32, fp32r, fp16, u32 = mybir.dt.float32, mybir.dt.float32r, mybir.dt.float16, mybir.dt.uint32
    ALU, ACT, AX = mybir.AluOpType, mybir.ActivationFunctionType, mybir.AxisListType

    NB, L, D = x_in.shape
    P = 128
    T = NB * L
    NT = T // P
    HD = 64
    DIM = w_out.shape[0]
    NPAIR = DIM // (2 * HD)
    KT = L // P
    NE, M = gate_w.shape[0], gate_proj.shape[2]
    MT = M // P
    EX = NE + 1
    UNITS = NB * NPAIR
    EPS = 1e-5
    SCALE = float(HD) ** -0.5
    SHIFT = 32.0

    x_tok = x_in.rearrange("n (t p) d -> p (n t) d", p=P)
    out_tok = out.rearrange("n (t p) d -> p (n t) d", p=P)

    ctx = ExitStack()
    with ctx:
        def sb(name, shape, dt):
            return ctx.enter_context(nc.sbuf_tensor(name, shape, dt))

        def sem(name):
            return ctx.enter_context(nc.semaphore(name))

        def bank(name, cols=512):
            return ctx.enter_context(nc.psum_tensor(name, [P, cols], fp32))

        def wait(eng, s, n):
            if not isinstance(n, int) or n > 0:
                eng.wait_ge(s, n)

        x_res = sb("x_res", [P, NT, D], fp32)
        xT = sb("xT", [P, 2, T], fp32r)
        xT_hi, xT_lo = xT[:, 0], xT[:, 1]
        yT = sb("yT", [P, T], fp32)
        xn = yT[:, :].rearrange("p (t d) -> p t d", d=D)
        R1 = sb("R1", [P, 14336], fp32r)
        QK = 2 * 2 * L
        qk = R1[:, 0:4 * QK].rearrange("p (b h s q) -> p b h s q", b=2, h=2, s=4)
        q1, q2, k1, k2 = (qk[:, :, :, j] for j in range(4))
        o = 4 * QK
        wqk = R1[:, o:o + 4096].rearrange("p (r s d) -> p r s d", r=NPAIR, s=4)
        wv_hi = R1[:, o + 4096:o + 5120]
        wv_lo = R1[:, o + 5120:o + 6144]
        WEX = 2 * 2 * M + 2 * MT * D
        w_ex = [R1[:, e * WEX:(e + 1) * WEX] for e in range(EX)]
        cT = R1[:, EX * WEX:EX * WEX + L]
        wo = sb("wo", [P, NPAIR, 2, D], fp32r)
        R2 = sb("R2", [P, 4096], fp32r)
        nat = R2[:, 0:2048].rearrange("p (s q) -> p s q", s=4)
        oT = R2[:, 2048:3072].rearrange("p (s q) -> p s q", s=2)
        r_wqk = R2[:, 3072:4096].rearrange("p (b s d) -> p b s d", b=2, s=4)
        h_sp = R2[:, :].rearrange("p (b s m q) -> p b s m q", b=2, s=2, m=MT)
        r_x = sb("r_x", [P, 2, D], fp32r)
        r_wo = sb("r_wo", [P, 2, 2, D], fp32r)
        r_b = sb("r_b", [P, 2, 2], fp32)
        VD = 2 * HD + 1
        r_v = sb("r_v", [P, KT, 2, 2, VD], fp16)
        m_row = sb("m_row", [KT, 2, P], fp32r)
        e32 = x_res[:, 0:16, :].rearrange("p (a t) d -> p a (t d)", a=2)
        o_sb = x_res[:, 16:16 + KT, :]
        prob = sb("prob", [P, 2, 2, KT, L], fp16)
        VW = 2 * KT * 2 * NPAIR
        v_all = sb("v_all", [P, VW * VD], fp16)
        v_hl = v_all[:, :].rearrange("p (t h d) -> p t h d", t=2 * KT, d=VD)
        v32 = v_all[:, :].bitcast(fp32)
        sq = prob[:, :, :, :, :].rearrange("p a b c d -> p (a b c d)").bitcast(fp32)
        mx = sb("mx", [P, 2, KT], fp32)
        rec = sb("rec", [P, KT], fp32)
        ident = sb("ident", [P, P], fp32)
        bqk = sb("bqk", [P, NPAIR, 2], fp32)
        bv = sb("bv", [P, NPAIR], fp32)
        bo = sb("bo", [P, 1], fp32)
        wb = sb("wb", [P, 1], fp32)
        mu = sb("mu", [P, NT], fp32)
        var = sb("var", [P, NT], fp32)
        rstd = sb("rstd", [P, NT], fp32)
        gwT = sb("gwT", [P, NE], fp32)
        beta_b = sb("beta_b", [P, NE], fp32)

        banks = [bank(f"bank{i}") for i in range(2)]
        s_bank = [bank(f"scores{i}", 1024) for i in range(2)]
        o_bank, x_bank = bank("o_bank"), bank("x_bank")

        s_x = [sem(f"x_in{g}") for g in range(4)]
        s_wraw, s_bias, s_small = sem("w_raw"), sem("bias_in"), sem("small_in")
        s_cst, s_whi, s_wsp = sem("constants"), sem("w_hi"), sem("w_split")
        s_wb = sem("wb_done")
        s_sum, s_mu, s_cen = sem("summed"), sem("mean"), sem("centred")
        s_sq, s_vsum, s_var, s_std, s_rstd = sem("squared"), sem("squares_summed"), sem("variance"), sem("std"), sem("rstd")
        s_xn, s_xn_last = sem("normalised"), sem("normalised_last")
        s_tr, s_xh, s_xl = sem("x_transposed"), sem("x_hi"), sem("x_lo")
        GT = NT // 4

        raw_w = v32[:, 0:3 * DIM]
        raw_wo = v32[:, 3 * DIM:3 * DIM + NPAIR * D].rearrange("p (r d) -> p r d", r=NPAIR)

        def grp(g):
            return slice(g * GT, (g + 1) * GT)

        def bc(t, g):
            return t[:, grp(g)].unsqueeze(2).to_broadcast([P, GT, D])

        def centre(dve, k, g):
            dve.reduce_sum(mu[:, grp(g)], x_res[:, grp(g), :], AX.X).then_inc(s_sum, 1)
            dve.wait_ge(s_sum, k + 1)
            dve.tensor_scalar(mu[:, grp(g)], mu[:, grp(g)], 1.0 / D, None, ALU.mult).then_inc(s_mu, 1)
            dve.wait_ge(s_mu, k + 1)
            dve.tensor_tensor(xn[:, grp(g), :], x_res[:, grp(g), :], bc(mu, g), ALU.subtract).then_inc(s_cen, 1)

        def square(act, k, g):
            act.wait_ge(s_cen, k + 1)
            act.activation(sq[:, g * GT * D:(g + 1) * GT * D],
                           yT[:, g * GT * D:(g + 1) * GT * D], ACT.Square).then_inc(s_sq, 1)

        def variance(dve, k, g):
            dve.wait_ge(s_sq, k + 1)
            dve.reduce_sum(var[:, grp(g)], sq[:, g * GT * D:(g + 1) * GT * D].rearrange("p (t d) -> p t d", d=D),
                           AX.X).then_inc(s_vsum, 1)
            dve.wait_ge(s_vsum, k + 1)
            dve.tensor_scalar(var[:, grp(g)], var[:, grp(g)], 1.0 / D, EPS, ALU.mult, ALU.add).then_inc(s_var, 1)

        def deviation(act, k, g):
            act.wait_ge(s_var, k + 1)
            act.activation(var[:, grp(g)], var[:, grp(g)], ACT.Sqrt).then_inc(s_std, 1)

        def inverse(dve, k, g):
            dve.wait_ge(s_std, k + 1)
            dve.reciprocal(rstd[:, grp(g)], var[:, grp(g)]).then_inc(s_rstd, 1)

        def normalise(eng, k, g, done):
            eng.wait_ge(s_rstd, k + 1)
            eng.tensor_tensor(xn[:, grp(g), :], xn[:, grp(g), :], bc(rstd, g), ALU.mult).then_inc(done, 1)

        t_banks = [banks[0], banks[1], s_bank[0][:, 0:L], s_bank[0][:, L:2 * L],
                   s_bank[1][:, 0:L], s_bank[1][:, L:2 * L], x_bank, o_bank]

        def block_at(order, j):
            return 2 * order[j // 2] + j % 2

        def t_bank_of(j):
            return t_banks[j % 7]

        def transpose_pe(pe, half, order, between=lambda: None):
            for j in range(NB):
                if j < 6:
                    pe.wait_ge(s_xn, 3 * half + j // 2 + 1)
                else:
                    pe.wait_ge(s_xn_last, half + 1)
                if j == 7:
                    pe.wait_ge(s_xl, NB * half + 1)
                if j == 4:
                    between()
                b = block_at(order, j)
                for t in range(KT):
                    last = pe.transpose(t_bank_of(j)[:, t * P:(t + 1) * P], xn[:, KT * b + t, :], ident[:, :])
                last.then_inc(s_tr, 1)

        def transpose_hi(act, half, order, js):
            for j in js:
                b = block_at(order, j)
                act.wait_ge(s_tr, NB * half + j + 1)
                act.activation(xT_hi[:, b * L:(b + 1) * L], t_bank_of(j)[:, :], ACT.Copy).then_inc(s_xh, 1)

        def transpose_lo(dve, half, order, js):
            for j in js:
                b = block_at(order, j)
                dve.wait_ge(s_xh, NB * half + j + 1)
                dve.tensor_tensor(xT_lo[:, b * L:(b + 1) * L], t_bank_of(j)[:, :],
                                  xT_hi[:, b * L:(b + 1) * L], ALU.subtract).then_inc(s_xl, 1)

        def layernorm_dve(dve, half, order, before):
            k = 4 * half
            before(0)
            centre(dve, k, order[0])
            before(1)
            centre(dve, k + 1, order[1])
            variance(dve, k, order[0])
            before(2)
            centre(dve, k + 2, order[2])
            inverse(dve, k, order[0])
            variance(dve, k + 1, order[1])
            before(3)
            centre(dve, k + 3, order[3])
            inverse(dve, k + 1, order[1])
            variance(dve, k + 2, order[2])
            transpose_lo(dve, half, order, (0, 1))
            inverse(dve, k + 2, order[2])
            variance(dve, k + 3, order[3])
            inverse(dve, k + 3, order[3])
            normalise(dve, k + 3, order[3], s_xn_last)
            transpose_lo(dve, half, order, range(2, NB))

        def layernorm_act(act, half, order, between):
            k = 4 * half
            square(act, k, order[0])
            square(act, k + 1, order[1])
            deviation(act, k, order[0])
            between(0)
            square(act, k + 2, order[2])
            deviation(act, k + 1, order[1])
            between(1)
            transpose_hi(act, half, order, (0, 1))
            square(act, k + 3, order[3])
            deviation(act, k + 2, order[2])
            between(2)
            transpose_hi(act, half, order, (2, 3))
            deviation(act, k + 3, order[3])
            between(3)
            transpose_hi(act, half, order, range(4, NB))

        ORDER1 = (0, 1, 2, 3)
        w_raw3 = raw_w.rearrange("p (s r d) -> p s r d", s=3, r=NPAIR)
        w_parts = [(wqk[:, :, 0, :], wqk[:, :, 1, :], w_raw3[:, 0]), (wqk[:, :, 2, :], wqk[:, :, 3, :], w_raw3[:, 1]),
                   (wv_hi.rearrange("p (r d) -> p r d", r=NPAIR), wv_lo.rearrange("p (r d) -> p r d", r=NPAIR), w_raw3[:, 2]),
                   (wo[:, :, 0, :], wo[:, :, 1, :], raw_wo)]

        def weight_lo(eng, n):
            hi, lo, raw = w_parts[n]
            eng.wait_ge(s_whi, n + 1)
            eng.tensor_tensor(lo, raw, hi, ALU.subtract).then_inc(s_wsp, 1)

        with nc.Block() as block:
            @block.sync
            def _(sp):
                for g in range(4):
                    sp.dma_start(x_res[:, grp(g), :], x_tok[:, grp(g), :]).then_inc(s_x[g], 16)
                sp.dma_start(raw_w, w_qkv).then_inc(s_wraw, 16)
                sp.dma_start(raw_wo, w_out.rearrange("(r p) d -> p r d", p=P)).then_inc(s_wraw, 16)
                with nc.allow_non_contiguous_dma(reason="biases by partition"):
                    for s in range(2):
                        sp.dma_start(bqk[:, :, s], b_qkv[s * DIM:(s + 1) * DIM].rearrange("(r p) -> p r", p=P)).then_inc(s_bias, 16)
                    sp.dma_start(bv[:, :], b_qkv[2 * DIM:].rearrange("(r p) -> p r", p=P)).then_inc(s_bias, 16)
                    sp.dma_start(bo[:, :], b_out.rearrange("(p o) -> p o", o=1)).then_inc(s_bias, 16)
                    sp.dma_start(gwT[:, :], gate_w.rearrange("e h -> h e")).then_inc(s_small, 16)
                    sp.dma_start(beta_b[:, :], beta.rearrange("(o e) -> o e", o=1).to_broadcast([P, NE])).then_inc(s_small, 16)

            @block.gpsimd
            def _(pool):
                pool.memset(ident[:, :], 0.0).then_inc(s_cst, 1)
                pool.wait_ge(s_cst, 1)
                pool.affine_select(out=ident[:, :], in_=ident[:, :], compare_op=ALU.not_equal, fill=1.0,
                                   base=0, pattern=[[-1, P]], channel_multiplier=1).then_inc(s_cst, 1)
                for i in range(3):
                    normalise(pool, i, ORDER1[i], s_xn)
                weight_lo(pool, 0)
                weight_lo(pool, 1)

            @block.vector
            def _(dve):
                dve.memset(k2[HD:HD + 1].bitcast(fp32), 1.0).then_inc(s_wb, 1)
                layernorm_dve(dve, 0, ORDER1, lambda i: dve.wait_ge(s_x[i], 16))
                weight_lo(dve, 2)
                weight_lo(dve, 3)
                dve.wait_ge(s_wb, 2)
                dve.wait_ge(s_bias, 64)
                dve.tensor_tensor(wb[:, :], o_bank[:, 0:1], bo[:, :], ALU.add).then_inc(s_cst, 1)

            @block.scalar
            def _(act):
                def weight_hi(n):
                    hi, _, raw = w_parts[n]
                    act.wait_ge(s_wraw, 32)
                    act.activation(hi, raw, ACT.Copy).then_inc(s_whi, 1)

                layernorm_act(act, 0, ORDER1, weight_hi)

            @block.tensor
            def _(pe):
                pe.wait_ge(s_cst, 2)
                transpose_pe(pe, 0, ORDER1)
                pe.wait_ge(s_wraw, 32)
                pe.wait_ge(s_bias, 64)
                for r in range(NPAIR):
                    last = pe.matmul(o_bank[:, 0:1], raw_wo[:, r, :], bv[:, r:r + 1], start=(r == 0), stop=(r == NPAIR - 1))
                last.then_inc(s_wb, 1)

        names = ("q_done k_done v_done ot_done y_done mt_done max_mm s_mm pv_mm exp_done q_hi k_hi v_hi "
                 "o_hi mrow q_lo k_lo v_lo o_lo maxed o_norm o_rec y_acc p_lo put0 put1 m_put0 m_put1 "
                 "ld_wqk ld_wo ld_x ld_v v_lo_first y_init v_ones")
        S = {n: sem(n) for n in names.split()}
        s_q, s_k, s_v, s_ot, s_y, s_mt = (S[n] for n in ("q_done", "k_done", "v_done", "ot_done", "y_done", "mt_done"))
        s_mm, s_sm, s_pv = S["max_mm"], S["s_mm"], S["pv_mm"]
        s_exp, s_qh, s_kh, s_vh, s_oh, s_mr = (S[n] for n in ("exp_done", "q_hi", "k_hi", "v_hi", "o_hi", "mrow"))
        s_ql, s_kl, s_vl, s_ol, s_mx, s_on, s_rec, s_ya = (
            S[n] for n in ("q_lo", "k_lo", "v_lo", "o_lo", "maxed", "o_norm", "o_rec", "y_acc"))
        s_pl, s_put, s_mp = S["p_lo"], (S["put0"], S["put1"]), (S["m_put0"], S["m_put1"])
        s_lw, s_lo, s_lx, s_lv = S["ld_wqk"], S["ld_wo"], S["ld_x"], S["ld_v"]
        s_yi, s_v1, s_vl0 = S["y_init"], S["v_ones"], S["v_lo_first"]
        V_UNITS = UNITS - NPAIR
        CH = NPAIR
        PUT = 3 * 16
        qv_bank, k_bank = banks
        max_bank = ((k_bank, qv_bank, x_bank, k_bank), (x_bank, qv_bank, k_bank, k_bank))
        v_bank = [b[:, s * L:(s + 1) * L] for b in s_bank for s in range(2)]

        def max_at(u, h, t):
            return v_bank[2 + t % 2] if isinstance(u, int) and u == 0 else max_bank[h][t]

        mt_rows = (x_bank[0:KT, 0:P], k_bank[0:KT, 0:P])

        def split3(pe, out_ap, sta_hi, sta_lo, mov_hi, mov_lo):
            pe.matmul(out_ap, sta_hi, mov_hi, start=True, stop=False)
            pe.matmul(out_ap, sta_hi, mov_lo, start=False, stop=False)
            return pe.matmul(out_ap, sta_lo, mov_hi, start=False, stop=True)

        def w_qk(u, par):
            return wqk[:, u] if isinstance(u, int) and u < 2 else r_wqk[:, par]

        def b_qk(u, par, s):
            b = bqk[:, u] if isinstance(u, int) and u < 2 else r_b[:, par]
            return b[:, s:s + 1]

        def pe_q(pe, u, par, x_hi, x_lo, before, n):
            wait(pe, before, n)
            wait(pe, s_lw, 32 * (u // 2))
            w = w_qk(u, par)
            split3(pe, qv_bank[:, :], w[:, 0], w[:, 1], x_hi, x_lo).then_inc(s_q, 1)

        def pe_k(pe, u, par, x_hi, x_lo, before, n):
            wait(pe, before, n)
            w = w_qk(u, par)
            split3(pe, k_bank[:, :], w[:, 2], w[:, 3], x_hi, x_lo).then_inc(s_k, 1)

        def pe_max(pe, u, par, h, t, before, n):
            if t == 0:
                pe.wait_ge(s_put[h], PUT * (u + 1))
            wait(pe, before, n)
            pe.matmul(max_at(u, h, t)[:, :], q1[:, par, h, t * P:(t + 1) * P], k1[:, par, h, :],
                      start=True, stop=True).then_inc(s_mm, 1)

        def pe_mt(pe, u, h):
            pe.wait_ge(s_mx, 8 * u + 4 * h + 4)
            pe.transpose(mt_rows[h], mx[:, h, :], ident[:, :]).then_inc(s_mt, 1)

        def pe_scores(pe, u, par, h, half):
            wait(pe, s_exp, 4 * u + 2 * h + half - 1)
            pe.wait_ge(s_mp[h], 16 * (u + 1))
            R = HD + 1
            for t in range(2):
                c = (2 * half + t) * P
                dst = s_bank[half][:, t * L:(t + 1) * L]
                pe.matmul(dst, k1[:, par, h, c:c + P], q1[:, par, h, :], start=True, stop=False)
                last = pe.matmul(dst, k2[0:R, par, h, c:c + P], q2[0:R, par, h, :], start=False, stop=True)
            last.then_inc(s_sm, 1)

        def pe_pv(pe, u, par, h, qs):
            if qs[0] == 0:
                pe.wait_ge(s_pl, 4 * u + 2 * h + 2)
                pe.wait_ge(s_lv, 16 * (u // 2 + 1))
                wait(pe, s_on, 2 * u + h)
            for q in qs:
                dst = o_bank[:, q * (HD + 1):(q + 1) * (HD + 1)]
                for t in range(KT):
                    hi = prob[:, 0, h, t, q * P:(q + 1) * P]
                    lo = prob[:, 1, h, t, q * P:(q + 1) * P]
                    v = r_v[:, t, par, h, :]
                    pe.matmul(dst, hi, v[:, 0:HD + 1], start=(t == 0), stop=False)
                    pe.matmul(dst[:, 0:HD], hi, v[:, HD + 1:], start=False, stop=False)
                    last = pe.matmul(dst, lo, v[:, 0:HD + 1], start=False, stop=(t == KT - 1))
            if qs[-1] == KT - 1:
                last.then_inc(s_pv, 1)

        def pe_ot(pe, u, before, n):
            wait(pe, before, n)
            pe.wait_ge(s_on, 2 * u + 2)
            for t in range(KT):
                last = pe.transpose(x_bank[:, t * P:(t + 1) * P], o_sb[:, t, :], ident[:, :])
            last.then_inc(s_ot, 1)

        def pe_y(pe, u, par):
            pe.wait_ge(s_ol, u + 1)
            pe.wait_ge(s_lo, 16 * (u // 2 + 1))
            split3(pe, x_bank[:, :], r_wo[:, par, 0], r_wo[:, par, 1], oT[:, 0], oT[:, 1]).then_inc(s_y, 1)

        def pe_v(pe, u, c, before, n):
            wait(pe, before, n)
            pe.wait_ge(s_lx, 16 * (u // 2 + 1))
            h = slice(c * L, (c + 1) * L)
            split3(pe, qv_bank[:, :], r_x[:, 0], r_x[:, 1], wv_hi[:, h], wv_lo[:, h]).then_inc(s_v, 1)

        def x_of(u, pe=None):
            n = (u // NPAIR) * L
            if isinstance(n, int):
                return xT_hi[:, n:n + L], xT_lo[:, n:n + L]
            n = pe.snap(n)
            return xT_hi[:, bass.ds(n, L)], xT_lo[:, bass.ds(n, L)]

        def pe_unit(pe, u, par, first=False, nxt=True, nxt2=True, v_too=True):
            v, g = u + 1, 8 * (u + 1)
            pe_scores(pe, u, par, 0, 1)
            if nxt:
                pe_max(pe, v, 1 - par, 0, 0, s_mr, 2 * v)
                pe_max(pe, v, 1 - par, 0, 1, *((s_mx, g) if first else (s_vl, 2 * u if v_too else 2 * V_UNITS)))
            if not first:
                pe_pv(pe, u - 1, 1 - par, 1, (0, 1))
            if nxt:
                pe_max(pe, v, 1 - par, 0, 2, *((s_mx, g) if first else (s_ya, u - 1)))
                pe_max(pe, v, 1 - par, 0, 3, s_mx, g + 1)
            if not first:
                pe_pv(pe, u - 1, 1 - par, 1, (2, 3))
            if nxt2:
                x_hi_lo = x_of(u + 2, pe)
                pe_q(pe, u + 2, par, *x_hi_lo, s_mx, g + 2)
            if nxt:
                pe_mt(pe, v, 0)
            if nxt2:
                pe_k(pe, u + 2, par, *x_hi_lo, s_mx, g + 4)
            pe_scores(pe, u, par, 1, 0)
            if nxt:
                pe_max(pe, v, 1 - par, 1, 0, s_mr, 2 * v + 1)
                pe_max(pe, v, 1 - par, 1, 1, *((s_ql, u + 3) if nxt2 else (s_mx, g + 2)))
            pe_scores(pe, u, par, 1, 1)
            if not first:
                pe_ot(pe, u - 1, *((s_mx, g + 5) if nxt else (s_ya, u - 1)))
            if nxt:
                pe_max(pe, v, 1 - par, 1, 2, *((s_kl, u + 3) if nxt2 else (s_mx, g + 4)))
            pe_pv(pe, u, par, 0, (0, 1))
            if v_too:
                pe_v(pe, u, par, s_mx, g + 6)
            if nxt:
                pe_max(pe, v, 1 - par, 1, 3, s_mx, g + 7)
            pe_pv(pe, u, par, 0, (2, 3))
            if nxt:
                pe_scores(pe, v, 1 - par, 0, 0)
                pe_mt(pe, v, 1)
            if not first:
                pe_y(pe, u - 1, 1 - par)

        def act_exp(act, u, h, half):
            act.wait_ge(s_sm, 4 * u + 2 * h + half + 1)
            wait(act, s_pl, 4 * u + 2 * h + half - 1)
            if half == 0:
                wait(act, s_pv, 2 * u + h - 1)
            act.activation(e32[:, half, :], s_bank[half][:, :], ACT.Exp, scale=SCALE)
            dst = prob[:, 0, h, 2 * half:2 * half + 2, :].rearrange("p t q -> p (t q)")
            act.activation(dst, s_bank[half][:, :], ACT.Exp, scale=SCALE).then_inc(s_exp, 1)

        def act_hi(act, u, par, s, done, own):
            act.wait_ge(done, u + 1)
            if s == 0:
                for h in range(2):
                    wait(act, s_put[h], PUT * u)
            act.activation(nat[:, 2 * s], banks[s][:, :], ACT.Identity, bias=b_qk(u, par, s)).then_inc(own, 1)

        def act_oh(act, u):
            act.wait_ge(s_ot, u + 1)
            wait(act, s_y, u)
            act.activation(oT[:, 0], x_bank[:, :], ACT.Copy).then_inc(s_oh, 1)

        def v_slot(u, c, part, eng=None):
            W = NPAIR * VD
            at = 2 * W * (((u // NPAIR + 1) % 2) * KT + (u % NPAIR) // 2) + c * W
            rows = v_all[:, at:at + W] if isinstance(u, int) else v_all[:, bass.ds(eng.snap(at), W)]
            return rows.rearrange("p (h d) -> p h d", d=VD)[:, :, slice(0, HD) if part == 0 else slice(HD + 1, VD)]

        x3 = qv_bank[:, :].rearrange("p (h d) -> p h d", d=HD)

        def act_vh(act, u, c):
            dst = v_slot(u, c, 0, act)
            act.wait_ge(s_v, CH + u + 1)
            act.activation(dst, x3, ACT.Copy).then_inc(s_vh, 1)

        def act_unit(act, u, par, first=False, nxt=True, nxt2=True, v_too=True):
            act_exp(act, u, 0, 0)
            act_exp(act, u, 0, 1)
            if nxt2:
                act_hi(act, u + 2, par, 0, s_q, s_qh)
                act_hi(act, u + 2, par, 1, s_k, s_kh)
            act_exp(act, u, 1, 0)
            if not first:
                act_oh(act, u - 1)
            act_exp(act, u, 1, 1)
            if v_too:
                act_vh(act, u, par)

        def dve_lo(dve, u, par, s, hi_done, own):
            dve.wait_ge(hi_done, u + 1)
            dve.scalar_tensor_tensor(out=nat[:, 2 * s + 1], in0=banks[s][:, :], scalar=b_qk(u, par, s),
                                     in1=nat[:, 2 * s].bitcast(fp32), op0=ALU.add, op1=ALU.subtract).then_inc(own, 1)

        def dve_max(dve, u, h, t):
            if t == 0:
                wait(dve, s_mt, 2 * u + h - 1)
            dve.wait_ge(s_mm, 8 * u + 4 * h + t + 1)
            dve.reduce_max(mx[:, h, t:t + 1], max_at(u, h, t)[:, :], AX.X).then_inc(s_mx, 1)

        def dve_mr(dve, u, h):
            dve.wait_ge(s_mt, 2 * u + h + 1)
            wait(dve, s_mp[h], 16 * u)
            dve.tensor_scalar(m_row[:, h, :], mt_rows[h], -1.0, SHIFT, ALU.mult, ALU.add).then_inc(s_mr, 1)

        def dve_norm(dve, u, h):
            dve.wait_ge(s_pv, 2 * u + h + 1)
            wait(dve, s_on, 2 * u + h)
            o3 = o_bank[:, 0:KT * (HD + 1)].rearrange("p (q d) -> p q d", d=HD + 1)
            dve.reciprocal(rec[:, :].unsqueeze(2), o3[:, :, HD:HD + 1]).then_inc(s_rec, 1)
            dve.wait_ge(s_rec, 2 * u + h + 1)
            wait(dve, s_ot, u)
            dve.tensor_tensor(o_sb[:, :, h * HD:(h + 1) * HD], o3[:, :, 0:HD],
                              rec[:, :].unsqueeze(2).to_broadcast([P, KT, HD]), ALU.mult).then_inc(s_on, 1)

        def dve_ol(dve, u):
            dve.wait_ge(s_oh, u + 1)
            wait(dve, s_y, u)
            dve.tensor_tensor(oT[:, 1], x_bank[:, :], oT[:, 0].bitcast(fp32), ALU.subtract).then_inc(s_ol, 1)

        def y_of(dve, u):
            n = (u // NPAIR) * L
            return yT[:, n:n + L] if isinstance(n, int) else yT[:, bass.ds(dve.snap(n), L)]

        def dve_ya(dve, u, y):
            dve.wait_ge(s_y, u + 1)
            dve.tensor_tensor(y, x_bank[:, :], y, ALU.add).then_inc(s_ya, 1)

        def dve_vl(dve, u, src, dst):
            dve.wait_ge(s_vh, CH + u + 1)
            dve.tensor_tensor(dst, x3, src, ALU.subtract).then_inc(s_vl, 2)

        def dve_unit(dve, u, par, first=False, nxt=True, nxt2=True, v_too=True):
            v = u + 1
            two_before = not (isinstance(u, int) and u < 2)
            if two_before:
                y = y_of(dve, u - 2)
                dve_ya(dve, u - 2, y)
            if nxt:
                for t in range(KT):
                    dve_max(dve, v, 0, t)
            if not first:
                dve_norm(dve, u - 1, 1)
            if nxt:
                dve_mr(dve, v, 0)
            if nxt2:
                dve_lo(dve, u + 2, par, 0, s_qh, s_ql)
            if nxt:
                dve_max(dve, v, 1, 0)
            if nxt2:
                dve_lo(dve, u + 2, par, 1, s_kh, s_kl)
            if nxt:
                dve_max(dve, v, 1, 1)
                dve_max(dve, v, 1, 2)
            if v_too:
                slots = v_slot(u, par, 0, dve), v_slot(u, par, 1, dve)
            if nxt:
                dve_max(dve, v, 1, 3)
            if not first:
                dve_ol(dve, u - 1)
            dve_norm(dve, u, 0)
            if nxt:
                dve_mr(dve, v, 1)
            if v_too:
                dve_vl(dve, u, *slots)

        def pool_unit(pool, u, par, first=False, nxt=True, nxt2=True, v_too=True):
            for h in range(2):
                for half in range(2):
                    pool.wait_ge(s_exp, 4 * u + 2 * h + half + 1)
                    if half == 0:
                        wait(pool, s_pv, 2 * u + h - 1)
                    view = lambda s: prob[:, s, h, 2 * half:2 * half + 2, :].rearrange("p t q -> p (t q)")
                    pool.tensor_tensor(view(1), e32[:, half, :], view(0), ALU.subtract).then_inc(s_pl, 1)

        def move(eng, dst, src):
            if src.dtype == fp32r:
                dst, src = dst.bitcast(fp32), src.bitcast(fp32)
            return eng.dma_start(dst, src)

        def put(sp, u, par, h):
            if h == 0:
                sp.wait_ge(s_kl, u + 1)
            if not (isinstance(u, int) and u < 2):
                sp.wait_ge(s_sm, 4 * (u - 2) + 2 * h + 2)
            A, B = slice(0, HD), slice(HD, P)
            src = (A, B)[h]
            move(sp, qk[A, par, h, 0:3], nat[src, 0:3]).then_inc(s_put[h], 16)
            move(sp, qk[B, par, h, 0:4:2], nat[src, 0:4:3]).then_inc(s_put[h], 16)
            move(sp, k2[A, par, h], nat[src, 2]).then_inc(s_put[h], 16)

        def put_m(sp, u, par, h):
            sp.wait_ge(s_mr, 2 * u + h + 1)
            move(sp, q2[HD:HD + 1, par, h, :], m_row[:, h, :]).then_inc(s_mp[h], 16)

        def two(t, n):
            return t[:, n:n + 2] if isinstance(n, int) else t[:, bass.ds(n, 2)]

        def ld_wqk(sp, u):
            if not (isinstance(u, int) and u == 2):
                sp.wait_ge(s_kl, u)
            move(sp, r_wqk, two(wqk, u % NPAIR)).then_inc(s_lw, 16)
            move(sp, r_b[:, :, :], two(bqk, u % NPAIR)).then_inc(s_lw, 16)

        def ld_wo(sp, u):
            wait(sp, s_y, u)
            move(sp, r_wo[:, :, :, :], two(wo, u % NPAIR)).then_inc(s_lo, 16)

        def ld_x(sp, u):
            if not (isinstance(u, int) and u == 0):
                sp.wait_ge(s_v, CH + u)
            t = ((u // NPAIR + 1) % NB) * KT + (u % NPAIR) // 2
            src = xT[:, :, t * P:(t + 1) * P] if isinstance(t, int) else xT[:, :, bass.ds(t * P, P)]
            move(sp, r_x[:, :, :], src).then_inc(s_lx, 16)

        def ld_v(sp, u, v_too):
            if isinstance(u, int) and u == 0:
                sp.wait_ge(s_vl0, CH)
            wait(sp, s_pv, 2 * u)
            wait(sp, s_vl, 2 * u if v_too else 2 * V_UNITS)
            n, r = u // NPAIR, u % NPAIR
            src = v_all[:, :].rearrange("p (b t r w) -> p b r t w", b=2, t=KT, r=NPAIR // 2)
            dst = r_v[:, :, :, :, :].rearrange("p t r h d -> p t (r h d)")
            if isinstance(u, int):
                src = src[:, n % 2, r // 2]
            else:
                src = src[:, bass.ds(n % 2, 1), bass.ds(r // 2, 1)].rearrange("p a b t w -> p (a b t) w")
            move(sp, dst, src).then_inc(s_lv, 16)

        def sp_unit(sp, u, par, first=False, nxt=True, nxt2=True, v_too=True):
            if par == 0:
                ld_v(sp, u, v_too)
            if nxt:
                put_m(sp, u + 1, 1 - par, 0)
            if nxt2:
                put(sp, u + 2, par, 0)
                if par == 1:
                    ld_wqk(sp, u + 3)
                put(sp, u + 2, par, 1)
                if par == 1 and v_too:
                    ld_x(sp, u + 1)
            if nxt:
                put_m(sp, u + 1, 1 - par, 1)
            if par == 0:
                ld_wo(sp, u)

        def run_units(eng, step):
            step(eng, 0, 0, first=True)
            step(eng, 1, 1)
            with eng.Fori(1, V_UNITS // 2) as i:
                step(eng, 2 * i, 0)
                step(eng, 2 * i + 1, 1)
            with eng.Fori(V_UNITS // 2, UNITS // 2 - 1) as i:
                step(eng, 2 * i, 0, v_too=False)
                step(eng, 2 * i + 1, 1, v_too=False)
            step(eng, UNITS - 2, 0, nxt2=False, v_too=False)
            step(eng, UNITS - 1, 1, nxt=False, nxt2=False, v_too=False)

        with nc.Block() as block:
            @block.sync
            def _(sp):
                ld_wqk(sp, 2)
                ld_x(sp, 0)
                put(sp, 0, 0, 0)
                put(sp, 0, 0, 1)
                put_m(sp, 0, 0, 0)
                put(sp, 1, 1, 0)
                put(sp, 1, 1, 1)
                put_m(sp, 0, 0, 1)
                sp.wait_ge(s_v1, 1)
                run_units(sp, sp_unit)
                sp.wait_ge(s_lw, 32 * (UNITS // 2))
                sp.wait_ge(s_lx, 16 * (V_UNITS // 2 + 1))

            @block.gpsimd
            def _(pool):
                pool.memset(v_hl[:, :, :, HD:HD + 1], 1.0).then_inc(s_v1, 1)
                pool.memset(yT[:, :], 0.0).then_inc(s_yi, 1)
                pool.wait_ge(s_yi, 1)
                pool.tensor_scalar(yT[:, :], yT[:, :], wb[:, 0:1], None, ALU.add).then_inc(s_yi, 1)
                run_units(pool, pool_unit)

            @block.scalar
            def _(act):
                act_hi(act, 0, 0, 0, s_q, s_qh)
                act_hi(act, 0, 0, 1, s_k, s_kh)
                for c in range(CH):
                    act.wait_ge(s_v, c + 1)
                    act.activation(v_hl[:, c // 2, (c % 2) * NPAIR:(c % 2 + 1) * NPAIR, 0:HD],
                                   v_bank[c % 4].rearrange("p (h d) -> p h d", d=HD), ACT.Copy).then_inc(s_vh, 1)
                act_hi(act, 1, 1, 0, s_q, s_qh)
                act_hi(act, 1, 1, 1, s_k, s_kh)
                run_units(act, act_unit)
                act_oh(act, UNITS - 1)

            @block.vector
            def _(dve):
                dve_lo(dve, 0, 0, 0, s_qh, s_ql)
                dve_lo(dve, 0, 0, 1, s_kh, s_kl)
                for c in range(CH):
                    dve.wait_ge(s_vh, c + 1)
                    h = slice((c % 2) * NPAIR, (c % 2 + 1) * NPAIR)
                    dve.tensor_tensor(v_hl[:, c // 2, h, HD + 1:], v_bank[c % 4].rearrange("p (h d) -> p h d", d=HD),
                                      v_hl[:, c // 2, h, 0:HD], ALU.subtract).then_inc(s_vl0, 1)
                for h in range(2):
                    for t in range(KT):
                        dve_max(dve, 0, h, t)
                    dve_mr(dve, 0, h)
                    if h == 0:
                        dve_lo(dve, 1, 1, 0, s_qh, s_ql)
                        dve_lo(dve, 1, 1, 1, s_kh, s_kl)
                dve.wait_ge(s_yi, 2)
                run_units(dve, dve_unit)
                dve_ya(dve, UNITS - 2, y_of(dve, UNITS - 2))
                dve_norm(dve, UNITS - 1, 1)
                dve_ol(dve, UNITS - 1)
                dve_ya(dve, UNITS - 1, y_of(dve, UNITS - 1))

            @block.tensor
            def _(pe):
                pe_q(pe, 0, 0, *x_of(0), s_ql, 0)
                pe_k(pe, 0, 0, *x_of(0), s_kl, 0)
                for c in range(CH):
                    if c >= 4:
                        pe.wait_ge(s_vl0, c - 3)
                    t = slice((c // 2) * P, (c // 2 + 1) * P)
                    h = slice((c % 2) * L, (c % 2 + 1) * L)
                    split3(pe, v_bank[c % 4], xT_hi[:, t], xT_lo[:, t], wv_hi[:, h], wv_lo[:, h]).then_inc(s_v, 1)
                pe_q(pe, 1, 1, *x_of(1), s_ql, 1)
                pe_k(pe, 1, 1, *x_of(1), s_kl, 1)
                pe.wait_ge(s_vl0, CH)
                for h in range(2):
                    for t in range(KT):
                        pe_max(pe, 0, 0, h, t, s_mx, 4 * h + t - 1)
                        if h == 1 and t == 1:
                            pe_scores(pe, 0, 0, 0, 0)
                    if h == 0:
                        pe_mt(pe, 0, 0)
                pe_mt(pe, 0, 1)
                run_units(pe, pe_unit)
                pe_pv(pe, UNITS - 1, 1, 1, range(KT))
                pe_ot(pe, UNITS - 1, s_ya, UNITS - 1)
                pe_y(pe, UNITS - 1, 1)

        s_yt, s_xr = sem("y_transposed"), sem("x_residual")
        s_lgT, s_lgc, s_lgp, s_lg = sem("logitsT"), sem("logitsT_copied"), sem("logits_done"), sem("logits_read")
        s_gws, s_rt, s_sg, s_sel = sem("gate_split"), sem("route_step"), sem("route_exp"), sem("select")
        s_wx, s_wxh, s_wxl = [sem(f"expert_raw{i}") for i in range(3)], sem("expert_hi"), sem("expert_lo")
        RAW = 3 * M
        gsp = wo[:, 0, 0, 0:2 * NE]
        sel = wo[:, 1:5, :, :].rearrange("p r s d -> p (r s) d")
        small = sq[:, 1024:3072]
        N8 = NT * NE
        lg, zb, mask, tmp, sig, cw = (small[:, j * N8:(j + 1) * N8].rearrange("p (t e) -> p t e", e=NE) for j in range(6))
        top = small[:, 6 * N8:7 * N8].rearrange("p (t e) -> p t e", e=NE)
        idx = small[:, 7 * N8:8 * N8].bitcast(u32).rearrange("p (t e) -> p t e", e=NE)
        cwk = zb
        c4 = sb("c4", [P, KT, NE], fp32)
        iota8 = sb("iota8", [P, NE], fp32)
        HT = NT // 2
        lgT = sq[0:2 * NE, 3072:3072 + 2 * L].rearrange("p (a q) -> p a q", a=2)
        lg_bank = (o_bank[0:2 * NE, :], t_banks[3][0:2 * NE, :])
        lt_bank = (t_banks[1][:, 0:2 * NE * HT], t_banks[2][:, 0:2 * NE * HT])
        ORDER2 = (3, 2, 0, 1)
        LAST = ORDER2[-1]
        selw = sq[:, LAST * NE * P:(LAST + 1) * NE * P].rearrange("p (e m) -> p e m", e=NE)
        w32 = v32[:, 0:EX * RAW].rearrange("p (e s d) -> p e s d", e=EX, s=3)
        WXG = ((0, NE // 2), (NE // 2, NE), (NE, EX))
        GONE = 16 + KT

        with nc.Block() as block:
            @block.sync
            def _(sp):
                for g, (a, b) in ((2, (2 * GT, GONE)), (0, (0, GT)), (1, (GT, 2 * GT))):
                    sp.dma_start(x_res[:, a:b, :], x_tok[:, a:b, :]).then_inc(s_x[g], 16)
                for i, (a, b) in enumerate(WXG):
                    g, u_, d_ = ((gate_proj[a:b], up_proj[a:b], down_proj[a:b]) if a < NE
                                 else (shared_gate, shared_up, shared_down))
                    sp.dma_start(w32[:, a:b, 0], g.rearrange("e p d -> p e d")).then_inc(s_wx[i], 16)
                    sp.dma_start(w32[:, a:b, 1], u_.rearrange("e p d -> p e d")).then_inc(s_wx[i], 16)
                    for k in range(MT):
                        sp.dma_start(w32[:, a:b, 2, k * D:(k + 1) * D],
                                     d_[:, k * P:(k + 1) * P, :].rearrange("e p d -> p e d")).then_inc(s_wx[i], 16)

            @block.gpsimd
            def _(pool):
                def expert_lo(es):
                    for e in es:
                        w = w_ex[e].rearrange("p (s k d) -> p s k d", s=3, k=2)
                        pool.wait_ge(s_wxh, e + 1)
                        pool.tensor_tensor(w[:, :, 1, :], w32[:, e], w[:, :, 0, :].bitcast(fp32), ALU.subtract).then_inc(s_wxl, 1)

                pool.wait_ge(s_small, 32)
                pool.tensor_copy(gsp[:, 0:NE], gwT[:, :]).then_inc(s_gws, 1)
                pool.wait_ge(s_gws, 1)
                pool.tensor_tensor(gsp[:, NE:], gwT[:, :], gsp[:, 0:NE].bitcast(fp32), ALU.subtract).then_inc(s_gws, 1)
                pool.iota(iota8[:, :], pattern=[[1, NE]], base=0, channel_multiplier=0,
                          allow_small_or_imprecise_dtypes=True).then_inc(s_gws, 1)
                pool.memset(cT.bitcast(fp32), 0.0).then_inc(s_sel, 1)
                pool.memset(selw, 0.0).then_inc(s_sel, 1)
                for n, base in enumerate((0, -32)):
                    pool.wait_ge(s_sel, 2 + n)
                    pool.affine_select(out=selw, in_=selw, compare_op=ALU.not_equal, fill=1.0, base=base,
                                       pattern=[[-1, NE], [0, P]], channel_multiplier=1).then_inc(s_sel, 1)
                pool.wait_ge(s_sel, 4)
                pool.tensor_copy(sel, selw).then_inc(s_sel, 1)
                expert_lo((0,))
                normalise(pool, 4, ORDER2[0], s_xn)
                expert_lo((1,))
                normalise(pool, 5, ORDER2[1], s_xn)
                normalise(pool, 6, ORDER2[2], s_xn)
                expert_lo(range(2, EX))

            @block.vector
            def _(dve):
                def residual(i):
                    for j in (2 * i, 2 * i + 1):
                        b = block_at(ORDER2, j)
                        dve.wait_ge(s_yt, j + 1)
                        if KT * b < GONE:
                            dve.wait_ge(s_x[b // 2], 32)
                        xs = x_res[:, KT * b:KT * (b + 1), :].rearrange("p t d -> p (t d)")
                        dve.tensor_tensor(xs, t_banks[j][:, :], xs, ALU.add).then_inc(s_xr, 1)
                    dve.wait_ge(s_xr, 2 * i + 2)

                layernorm_dve(dve, 1, ORDER2, residual)
                n = [0]

                def step(ins):
                    ins.then_inc(s_rt, 1)
                    n[0] += 1
                    dve.wait_ge(s_rt, n[0])

                def route(half):
                    ts = slice(HT, NT) if half == 0 else slice(0, HT)
                    z, to, m_, tm, sg, lh = zb[:, ts, :], top[:, ts, :], mask[:, ts, :], tmp[:, ts, :], sig[:, ts, :], lg[:, ts, :]
                    dve.wait_ge(s_lgp, NB // 2 * (half + 1))
                    l3 = lt_bank[half].rearrange("p (t e) -> p t e", e=2 * NE)
                    dve.tensor_copy(lh, l3[:, :, 0:NE]).then_inc(s_lg, 1)
                    dve.wait_ge(s_lg, 2 * half + 1)
                    dve.tensor_tensor(lh, l3[:, :, NE:], lh, ALU.add).then_inc(s_lg, 1)
                    dve.wait_ge(s_lg, 2 * half + 2)
                    step(dve.tensor_tensor(z, lh, beta_b[:, :].unsqueeze(1).to_broadcast([P, HT, NE]), ALU.add))
                    for t in range(HT):
                        last = dve.max(to[:, t, :], z[:, t, :])
                    step(last)
                    for t in range(HT):
                        last = dve.max_index(idx[:, ts.start + t, :], to[:, t, :], z[:, t, :])
                    step(last)
                    step(dve.tensor_copy(tm, idx[:, ts, :]))
                    io = iota8[:, :].unsqueeze(1).to_broadcast([P, HT, NE])
                    step(dve.tensor_tensor(m_, io, tm[:, :, 0:1].to_broadcast([P, HT, NE]), ALU.is_equal))
                    step(dve.tensor_tensor(to, io, tm[:, :, 1:2].to_broadcast([P, HT, NE]), ALU.is_equal))
                    step(dve.tensor_tensor(m_, m_, to, ALU.add))
                    dve.wait_ge(s_sg, half + 1)
                    step(dve.tensor_scalar(sg, sg, 1.0, None, ALU.add))
                    step(dve.reciprocal(cw[:, ts, :], sg))
                    step(dve.tensor_tensor(cwk[:, ts, :], cw[:, ts, :], m_, ALU.mult))

                dve.wait_ge(s_small, 32)
                dve.wait_ge(s_gws, 3)
                for half in range(2):
                    route(half)

            @block.scalar
            def _(act):
                def expert_hi(es):
                    for e in es:
                        i = min(e // (NE // 2), 2)
                        w = w_ex[e].rearrange("p (s k d) -> p s k d", s=3, k=2)
                        act.wait_ge(s_wx[i], 16 * (2 + MT))
                        act.activation(w[:, :, 0, :], w32[:, e], ACT.Copy).then_inc(s_wxh, 1)

                def between(n):
                    expert_hi(((0,), (1, 2), (3, 4), ())[n])
                    if n == 1:
                        act.wait_ge(s_sel, 5)

                def logits_copy(js):
                    for j in js:
                        act.wait_ge(s_lgT, j + 1)
                        wait(act, s_lgp, j - 1)
                        act.activation(lgT[:, j % 2], lg_bank[j % 2], ACT.Copy).then_inc(s_lgc, 1)

                def exp_logits(half):
                    ts = slice(HT, NT) if half == 0 else slice(0, HT)
                    act.wait_ge(s_lg, 2 * half + 2)
                    act.activation(sig[:, ts, :], lg[:, ts, :], ACT.Exp, scale=-1.0).then_inc(s_sg, 1)

                layernorm_act(act, 1, ORDER2, between)
                logits_copy(range(NB // 2))
                expert_hi((5,))
                logits_copy(range(NB // 2, NB))
                expert_hi((6, 7))
                exp_logits(0)
                expert_hi((8,))
                exp_logits(1)

            @block.tensor
            def _(pe):
                for j in range(NB):
                    for t in range(KT):
                        c = block_at(ORDER2, j) * L + t * P
                        last = pe.transpose(t_banks[j][:, t * P:(t + 1) * P], yT[:, c:c + P], ident[:, :])
                    last.then_inc(s_yt, 1)

                def logits(j):
                    b = block_at(ORDER2, j)
                    pe.wait_ge(s_xl, NB + max(j, 3 if j % 2 else 0) + 1)
                    wait(pe, s_lgc, j - 1)
                    dst = lg_bank[j % 2]
                    pe.matmul(dst, gsp, xT_hi[:, b * L:(b + 1) * L], start=True, stop=False)
                    pe.matmul(dst, gsp, xT_lo[:, b * L:(b + 1) * L], start=False, stop=True).then_inc(s_lgT, 1)

                def by_tokens(j):
                    b = block_at(ORDER2, j)
                    pe.wait_ge(s_lgc, j + 1)
                    for t in range(KT):
                        c = 2 * NE * ((KT * b + t) % HT)
                        last = pe.transpose(lt_bank[j // 4][:, c:c + 2 * NE], lgT[:, j % 2, t * P:(t + 1) * P],
                                            ident[0:2 * NE, 0:2 * NE])
                    last.then_inc(s_lgp, 1)

                pe.wait_ge(s_gws, 2)
                transpose_pe(pe, 1, ORDER2, lambda: logits(0))
                for j in range(1, NB):
                    logits(j)
                    by_tokens(j - 1)
                by_tokens(NB - 1)

        names = ("c_copied c_transposed c_hi c_lo c_bcast c_read g_done u_done silu sc_done h_done h_hi h_lo "
                 "down_done y_read yt_done out_done out_put")
        S = {n: sem("m_" + n) for n in names.split()}
        m = S
        sl = yT[:, 0:2 * L].rearrange("p (m q) -> p m q", m=MT)
        sc = yT[:, 2 * L:4 * L].rearrange("p (m q) -> p m q", m=MT)
        hf = yT[:, 4 * L:6 * L].rearrange("p (m q) -> p m q", m=MT)
        cb = yT[:, 6 * L:8 * L].rearrange("p (b q) -> p b q", b=2)
        y_sb = sq[:, 2048:2048 + L]
        o_out = sq[:, 2560:2560 + 2 * L].rearrange("p (b q) -> p b q", b=2)
        g_bank = [s_bank[0][:, 0:L], s_bank[0][:, L:2 * L]]
        u_bank = [s_bank[1][:, 0:L], s_bank[1][:, L:2 * L]]
        c_bank, y_bank, t_bank = banks[0], banks[1], o_bank
        KC = 40

        def w_of(e):
            w = w_ex[e].rearrange("p (s k d) -> p s k d", s=3, k=2)
            return w[:, 0], w[:, 1], w[:, 2].rearrange("p k (m d) -> p k m d", m=MT)

        def blocks(eng, block_of):
            block_of(eng, 0, first=True)
            with eng.Fori(1, NB - 1) as b:
                block_of(eng, b)
            block_of(eng, NB - 1, final=True)

        def up(pe, b, e):
            n = EX * b + e
            if e < NE:
                if e == 0:
                    wait(pe, m["c_lo"], b + 1)
                wait(pe, m["c_read"], NE * b + e)
                pe.matmul(c_bank[:, :], sel[0:KC, e, :], cT[0:KC, :], start=True, stop=True).then_inc(m["c_bcast"], 1)
            hi, lo = xT_hi[:, bass.ds(b * L, L)], xT_lo[:, bass.ds(b * L, L)]
            wg, wu, _ = w_of(e)
            for k in range(MT):
                c = slice(k * P, (k + 1) * P)
                wait(pe, m["silu"], MT * (n - 1) + k + 1)
                split3(pe, g_bank[k], wg[:, 0, c], wg[:, 1, c], hi, lo).then_inc(m["g_done"], 1)
                wait(pe, m["h_done"], MT * (n - 1) + k + 1)
                split3(pe, u_bank[k], wu[:, 0, c], wu[:, 1, c], hi, lo).then_inc(m["u_done"], 1)

        def down(pe, b, e):
            n = EX * b + e
            if e == 0:
                wait(pe, m["y_read"], b)
            wd = w_of(e)[2]
            hs = h_sp[:, e % 2]
            for k in range(MT):
                wait(pe, m["h_lo"], MT * n + k + 1)
                first, final = e == 0 and k == 0, e == EX - 1 and k == MT - 1
                pe.matmul(y_bank[:, :], wd[:, 0, k], hs[:, 0, k], start=first, stop=False)
                pe.matmul(y_bank[:, :], wd[:, 0, k], hs[:, 1, k], start=False, stop=False)
                last = pe.matmul(y_bank[:, :], wd[:, 1, k], hs[:, 0, k], start=False, stop=final)
            last.then_inc(m["down_done"], 1)

        def c_transpose(pe, b):
            wait(pe, m["c_copied"], b + 1)
            wait(pe, m["out_done"], b - 1)
            for t in range(KT):
                last = pe.transpose(t_bank[0:NE, t * P:(t + 1) * P], c4[:, t, :], ident[:, :])
            last.then_inc(m["c_transposed"], 1)

        def y_transpose(pe, b):
            wait(pe, m["y_read"], b + 1)
            if not (isinstance(b, int) and b == NB - 1):
                wait(pe, m["c_lo"], b + 1)
            for t in range(KT):
                last = pe.transpose(t_bank[:, t * P:(t + 1) * P], y_sb[:, t * P:(t + 1) * P], ident[:, :])
            last.then_inc(m["yt_done"], 1)

        with nc.Block() as block:
            @block.tensor
            def _(pe):
                def block_of(pe, b, first=False, final=False):
                    for e in range(EX):
                        if e == 5 and not final:
                            c_transpose(pe, b + 1)
                        up(pe, b, e)
                        if e == 1 and not first:
                            y_transpose(pe, b - 1)
                        if e >= 1:
                            down(pe, b, e - 1)
                        elif not first:
                            down(pe, b - 1, EX - 1)

                c_transpose(pe, 0)
                blocks(pe, block_of)
                down(pe, NB - 1, EX - 1)
                y_transpose(pe, NB - 1)

            @block.scalar
            def _(act):
                def high(b, e, k):
                    n = EX * b + e
                    wait(act, m["h_done"], MT * n + k + 1)
                    wait(act, m["down_done"], n - 1 if e else n)
                    act.activation(h_sp[:, e % 2, 0, k], hf[:, k], ACT.Copy).then_inc(m["h_hi"], 1)

                def c_high(b):
                    wait(act, m["c_transposed"], b + 1)
                    wait(act, m["c_bcast"], NE * b)
                    act.activation(cT[0:NE, :], t_bank[0:NE, :], ACT.Copy).then_inc(m["c_hi"], 1)

                def y_out(b):
                    wait(act, m["down_done"], EX * (b + 1))
                    wait(act, m["yt_done"], b)
                    act.activation(y_sb, y_bank[:, :], ACT.Copy).then_inc(m["y_read"], 1)

                def block_of(act, b, first=False, final=False):
                    for e in range(EX):
                        n = EX * b + e
                        if e < NE:
                            wait(act, m["c_bcast"], NE * b + e + 1)
                            wait(act, m["sc_done"], MT * (NE * b + e - 1))
                            act.activation(cb[:, e % 2], c_bank[:, :], ACT.Copy).then_inc(m["c_read"], 1)
                        if e == EX - 1 and not final:
                            c_high(b + 1)
                        for k in range(MT):
                            if k == 1 and e >= 1:
                                high(b, e - 1, 1)
                            elif k == 1 and not first:
                                high(b - 1, EX - 1, 1)
                            if k == 1 and e == 1 and not first:
                                y_out(b - 1)
                            wait(act, m["g_done"], MT * n + k + 1)
                            if e >= 1:
                                wait(act, m["sc_done"], MT * (NE * b + e - 1) + k + 1)
                            else:
                                wait(act, m["h_done"], MT * (n - 1) + k + 1)
                            act.activation(sl[:, k], g_bank[k], ACT.Silu).then_inc(m["silu"], 1)
                        high(b, e, 0)

                c_high(0)
                blocks(act, block_of)
                high(NB - 1, EX - 1, 1)
                y_out(NB - 1)

            @block.gpsimd
            def _(pool):
                def block_of(pool, b, first=False, final=False):
                    for e in range(NE):
                        n = EX * b + e
                        wait(pool, m["c_read"], NE * b + e + 1)
                        for k in range(MT):
                            wait(pool, m["silu"], MT * n + k + 1)
                            wait(pool, m["h_done"], MT * (n - 1 if e else n - 2) + k + 1)
                            pool.tensor_tensor(sc[:, k], sl[:, k], cb[:, e % 2], ALU.mult).then_inc(m["sc_done"], 1)

                blocks(pool, block_of)

            @block.vector
            def _(dve):
                def low(b, e, k):
                    n = EX * b + e
                    wait(dve, m["h_hi"], MT * n + k + 1)
                    hs = h_sp[:, e % 2]
                    dve.tensor_tensor(hs[:, 1, k], hf[:, k], hs[:, 0, k].bitcast(fp32), ALU.subtract).then_inc(m["h_lo"], 1)

                def c_copy(b):
                    wait(dve, m["c_transposed"], b)
                    src = cwk[:, bass.ds(KT * b, KT), :]
                    dve.tensor_copy(c4[:, :, :], src).then_inc(m["c_copied"], 1)

                def c_low(b):
                    wait(dve, m["c_hi"], b + 1)
                    dve.tensor_tensor(cT[32:32 + NE, :], t_bank[0:NE, :], cT[0:NE, :].bitcast(fp32),
                                      ALU.subtract).then_inc(m["c_lo"], 1)

                def out(b):
                    xs = x_res[:, bass.ds(KT * b, KT), :].rearrange("p t d -> p (t d)")
                    wait(dve, m["yt_done"], b + 1)
                    wait(dve, m["out_put"], 16 * b)
                    dve.tensor_tensor(o_out[:, 0], t_bank[:, :], xs, ALU.add).then_inc(m["out_done"], 1)

                def block_of(dve, b, first=False, final=False):
                    for e in range(EX):
                        n = EX * b + e
                        if e == EX - 1 and not final:
                            c_low(b + 1)
                        for k in range(MT):
                            wait(dve, m["u_done"], MT * n + k + 1)
                            if e < NE:
                                wait(dve, m["sc_done"], MT * (NE * b + e) + k + 1)
                            else:
                                wait(dve, m["silu"], MT * n + k + 1)
                            wait(dve, m["h_lo"], MT * (n - 1) + k + 1)
                            src = sc if e < NE else sl
                            dve.tensor_tensor(hf[:, k], u_bank[k], src[:, k], ALU.mult).then_inc(m["h_done"], 1)
                        for k in range(MT):
                            low(b, e, k)
                        if e == 1 and not first:
                            out(b - 1)
                        if e == 3 and not final:
                            c_copy(b + 1)

                c_copy(0)
                c_low(0)
                blocks(dve, block_of)
                out(NB - 1)

            @block.sync
            def _(sp):
                def block_of(sp, b, first=False, final=False):
                    wait(sp, m["out_done"], b + 1)
                    sp.dma_start(out_tok[:, bass.ds(KT * b, KT), :],
                                 o_out[:, 0].rearrange("p (t d) -> p t d", d=D)).then_inc(m["out_put"], 16)

                blocks(sp, block_of)
                sp.wait_ge(m["out_put"], 16 * NB)


_INS = ["L0_attn_data", "L0_attn_W_qkv", "L0_attn_b_qkv", "L0_attn_W_out", "L0_attn_b_out", "L0_ffn_gate_w",
        "L0_ffn_beta", "L0_ffn_gate_proj_w", "L0_ffn_up_proj_w", "L0_ffn_down_proj_w", "L0_ffn_shared_gate_w",
        "L0_ffn_shared_up_w", "L0_ffn_shared_down_w"]
_OUT = ((8, 512, 128), "float32")


def kernel(**inputs):
    import numpy as _np
    import concourse.bacc as _bacc
    from concourse import mybir as _mybir
    from concourse.bass_utils import run_bass_kernel_spmd as _run

    nc = _bacc.Bacc("TRN2", target_bir_lowering=False, num_devices=1)
    arrays, args = {}, []
    for name in _INS:
        a = _np.ascontiguousarray(inputs[name])
        arrays[f"in_{name}_dram"] = a
        args.append(nc.dram_tensor(f"in_{name}_dram", a.shape, _mybir.dt.from_np(a.dtype), kind="ExternalInput").ap())
    shape, dtype = _OUT
    args.append(nc.dram_tensor("out_dram", shape, _mybir.dt.from_np(_np.dtype(dtype)), kind="ExternalOutput").ap())
    preln_attention_moe_kernel(nc, *args)
    r = _run(nc, [arrays], core_ids=[0])
    return r.results[0]["out_dram"]
```
